# Optimizing a Trainium2 kernel written in Bass

```python
import numpy as np
import jax
import jax.numpy as jnp

def _softmax(x, axis=-1):
    return jax.nn.softmax(x, axis=axis)

def _gelu(x):
    return jax.nn.gelu(x, approximate=True)

def _silu(x):
    return jax.nn.silu(x)

def _sigmoid(x):
    return jax.nn.sigmoid(x)

def _layernorm(x, axis=-1, eps=1e-05):
    m = jnp.mean(x, axis=axis, keepdims=True)
    v = jnp.var(x, axis=axis, keepdims=True)
    return (x - m) / jnp.sqrt(v + eps)

def _scatter_add(tgt, idx, src, axis=0):
    return tgt.at[idx].add(src)

def _segment_sum(src, seg, n):
    return jax.ops.segment_sum(src, seg, n)
kernel_name = 'mk_adaln_ffn_d1_seqx_r4_3d3f42'

def setup_inputs(seed: int=0):
    np.random.seed(seed)
    _w = jnp.asarray

    def _rec_inputs():
        import jax
        import jax.numpy as jnp
        _rk = jax.random.key(seed)
        x = -0.0002928 + 1 * jax.random.normal(jax.random.fold_in(_rk, 1), (64, 64, 256), jnp.float32)
        _lenS = 64 - jax.random.randint(jax.random.fold_in(_rk, 7), (64,), 0, max(1, 64 // 4) + 1, jnp.int32)
        _lenS2 = 64 - jax.random.randint(jax.random.fold_in(_rk, 8), (64,), 0, max(1, 64 // 4) + 1, jnp.int32)
        cond_256 = -0.106481 + 1.03144 * jax.random.normal(jax.random.fold_in(_rk, 11), (64, 64), jnp.float32)
        return (x, cond_256)
    x, cond_256 = _rec_inputs()

    def _L0_cond_setup():
        import jax, jax.numpy as jnp
        import numpy as np
        TOP_K = 2
        EPS = 1e-06
        B, S, H, G, E, M = (2, 512, 256, 64, 8, 512)
        key = jax.random.key(seed)
        ks = jax.random.split(key, 16)
        s_h = 1.0 / np.sqrt(H)
        s_g = 1.0 / np.sqrt(G)
        s_m = 1.0 / np.sqrt(M)
        return {'x': jax.random.normal(ks[0], (B, S, H), jnp.float32), 'genre_embed': jax.random.normal(ks[1], (B, 1, G), jnp.float32), 'rms_w': jnp.ones((H,), jnp.float32), 'wg_W': jax.random.normal(ks[2], (H, E), jnp.float32) * s_h, 'wg_b': jnp.zeros((E,), jnp.float32), 'gg_W': jax.random.normal(ks[3], (G, E), jnp.float32) * s_g, 'gg_b': jnp.zeros((E,), jnp.float32), 'W1': jax.random.normal(ks[4], (E, H, M), jnp.float32) * s_h, 'b1': jnp.zeros((E, M), jnp.float32), 'W2': jax.random.normal(ks[5], (E, M, M), jnp.float32) * s_m, 'b2': jnp.zeros((E, M), jnp.float32), 'W3': jax.random.normal(ks[6], (E, M, H), jnp.float32) * s_m, 'b3': jnp.zeros((E, H), jnp.float32)}
    _L0_cond_all = _L0_cond_setup()
    _L0_cond_in = {k: v for k, v in _L0_cond_all.items() if k in ('rms_w', 'wg_W', 'wg_b', 'gg_W', 'gg_b', 'W1', 'b1', 'W2', 'b2', 'W3', 'b3')}
    del _L0_cond_all

    def _L0_ffn_setup():
        import jax, jax.numpy as jnp
        import numpy as np
        IN_FEATURES = 256
        OUT_FEATURES = 256
        B, S = (8, 1024)
        key = jax.random.key(seed)
        kx, kw = jax.random.split(key)
        x = jax.random.normal(kx, (B, S, IN_FEATURES), dtype=jnp.float32)
        weight = jax.random.normal(kw, (OUT_FEATURES, IN_FEATURES), dtype=jnp.float32) * 0.1
        bias = jnp.zeros((OUT_FEATURES,), dtype=jnp.float32)
        return {'x': x, 'weight': weight, 'bias': bias}
    _L0_ffn_all = _L0_ffn_setup()
    _L0_ffn_in = {k: v for k, v in _L0_ffn_all.items() if k in ('weight', 'bias')}
    del _L0_ffn_all
    return {'x': x, 'cond_256': cond_256, 'L0_cond_rms_w': _L0_cond_in['rms_w'], 'L0_cond_wg_W': _L0_cond_in['wg_W'], 'L0_cond_wg_b': _L0_cond_in['wg_b'], 'L0_cond_gg_W': _L0_cond_in['gg_W'], 'L0_cond_gg_b': _L0_cond_in['gg_b'], 'L0_cond_W1': _L0_cond_in['W1'], 'L0_cond_b1': _L0_cond_in['b1'], 'L0_cond_W2': _L0_cond_in['W2'], 'L0_cond_b2': _L0_cond_in['b2'], 'L0_cond_W3': _L0_cond_in['W3'], 'L0_cond_b3': _L0_cond_in['b3'], 'L0_ffn_weight': _L0_ffn_in['weight'], 'L0_ffn_bias': _L0_ffn_in['bias']}

def reference(x, cond_256, L0_cond_rms_w, L0_cond_wg_W, L0_cond_wg_b, L0_cond_gg_W, L0_cond_gg_b, L0_cond_W1, L0_cond_b1, L0_cond_W2, L0_cond_b2, L0_cond_W3, L0_cond_b3, L0_ffn_weight, L0_ffn_bias):
    import jax
    import jax.numpy as jnp

    def _L0_cond_ref(x, genre_embed, rms_w, wg_W, wg_b, gg_W, gg_b, W1, b1, W2, b2, W3, b3):
        import jax, jax.numpy as jnp
        import numpy as np
        TOP_K = 2
        EPS = 1e-06
        E = W1.shape[0]
        var = jnp.mean(x * x, axis=-1, keepdims=True)
        xn = rms_w * (x * jax.lax.rsqrt(var + EPS))
        gate = xn @ wg_W + wg_b + (genre_embed @ gg_W + gg_b)
        gate_w = jax.nn.softmax(gate, axis=-1)
        topk_w, topk_i = jax.lax.top_k(gate_w, TOP_K)
        cw = jnp.sum(jax.nn.one_hot(topk_i, E, dtype=x.dtype) * topk_w[..., None], axis=-2)
        h1 = jax.nn.relu(jnp.einsum('bsh,ehm->bsem', x, W1) + b1)
        h2 = jax.nn.relu(jnp.einsum('bsem,emn->bsen', h1, W2) + b2)
        out_e = jnp.einsum('bsen,enh->bseh', h2, W3) + b3
        return jnp.einsum('bseh,bse->bsh', out_e, cw)

    def _L0_ffn_ref(x, weight, bias):
        import jax, jax.numpy as jnp
        import numpy as np
        IN_FEATURES = 256
        OUT_FEATURES = 256
        B, S = (8, 1024)
        w_scale = jnp.mean(jnp.abs(weight))
        q_weight = jnp.sign(weight) * (jnp.abs(weight) > 0.5 * w_scale).astype(weight.dtype)
        i_scale = jnp.max(jnp.abs(x)) / 127.0
        q_input = jnp.clip(jnp.round(x / i_scale), -128.0, 127.0)
        out = jnp.einsum('bsk,ok->bso', q_input, q_weight) * w_scale * i_scale
        out = out + bias
        return out
    x = x + _L0_ffn_ref(_L0_cond_ref(x, cond_256[:, None, :], L0_cond_rms_w, L0_cond_wg_W, L0_cond_wg_b, L0_cond_gg_W, L0_cond_gg_b, L0_cond_W1, L0_cond_b1, L0_cond_W2, L0_cond_b2, L0_cond_W3, L0_cond_b3), L0_ffn_weight, L0_ffn_bias)
    return x

_drawn_inputs = setup_inputs


def setup_inputs(seed=0):
    import zlib

    import numpy as np

    out = dict(_drawn_inputs(seed))
    spreads = {'L0_cond_rms_w': (1.0, 0.2),
     'L0_cond_wg_b': (0.0, 0.1),
     'L0_cond_gg_b': (0.0, 0.1),
     'L0_cond_b1': (0.0, 0.294),
     'L0_cond_b2': (0.0, 0.1),
     'L0_cond_b3': (0.0, 0.1),
     'L0_ffn_bias': (0.0, 0.1)}
    factors = {}
    for name, (base, spread) in spreads.items():
        noise = np.random.default_rng([zlib.crc32(name.encode()), seed]).standard_normal(out[name].shape)
        drawn = base * np.exp(spread * noise) if base else spread * noise
        out[name] = jnp.asarray(drawn.astype(out[name].dtype))
    for name, factor in factors.items():
        out[name] = (out[name] * factor).astype(out[name].dtype)
    return out
```

```python
from contextlib import ExitStack

import concourse.bass as bass
from concourse import mybir

P = 128
ALU = mybir.AluOpType
ACT = mybir.ActivationFunctionType
AX = mybir.AxisListType
F32 = mybir.dt.float32
BF16 = mybir.dt.bfloat16
I32 = mybir.dt.int32
U32 = mybir.dt.uint32
MAGIC = 12582912.0


def moe_ffn(nc, x, xT, condT, rms, wg, wgb, gg, ggb, w, b1, b2, b3, fwT, fbias, out):
    T, H = x.shape
    E = wg.shape[1]
    M = b1.shape[1]
    NB = condT.shape[1]
    G = condT.shape[0]
    C = T // P
    HK, MK = H // P, M // P
    WE = HK * M + MK * M + MK * H
    W2O, W3O = HK * M, HK * M + MK * M
    NT = (2 * T + E * (P - 1)) // P
    DUMMY = 2 * T
    CW = C * E
    SB = T // NB
    assert C * 2 == NB and SB * 2 == P and HK == 2 and MK == 4

    with ExitStack() as ctx:
        def sb(name, shape, dt=F32):
            return ctx.enter_context(nc.sbuf_tensor(name, shape, dt))

        def sem(name):
            return ctx.enter_context(nc.semaphore(name))

        pair_rows = nc.dram_tensor("pair_rows", [2 * T + 2 * P, H], F32, kind="Internal").ap()

        arena = sb("arena", [P, E * WE])

        def area(expert, words):
            return arena[:, expert * WE:expert * WE + words]

        x_tok = area(4, C * H)
        x_feat = area(6, HK * T).rearrange("p (k t) -> p k t", k=HK)
        half = C * P // 2
        onehot_r, onehot_t = [], []
        for k in range(2):
            base = (4 + 2 * k) * WE
            onehot_r.append(arena[:, base:base + half].bitcast(BF16).rearrange("p (c r) -> p c r", c=C))
            onehot_t.append(arena[:, base + half:base + half + C * NT].bitcast(BF16)
                            .rearrange("p (c v t) -> p c v t", c=C, v=2))
        y_low = area(0, C * H)
        y_high = area(2, C * H)
        x_res = area(4, C * H)

        CG = 4
        NG = C // CG
        scratch = sb("scratch", [P, 4 * CG * H])
        q16 = [scratch[:, n * CG * H // 2:(n + 1) * CG * H // 2].bitcast(BF16) for n in range(2)]
        qT = [scratch[:, (n + 2) * CG * H // 2:(n + 3) * CG * H // 2].bitcast(BF16) for n in range(2)]
        res = [scratch[:, (n + 2) * CG * H:(n + 3) * CG * H] for n in range(2)]
        taken = [0]

        def tmp(words):
            taken[0] += words
            assert taken[0] <= scratch.shape[1]
            return scratch[:, taken[0] - words:taken[0]]

        take_now = [sb(f"take_now{n}", [P, 1], I32) for n in range(2)]
        put_now = [sb(f"put_now{n}", [P, 1], I32) for n in range(2)]
        rows = [sb(f"rows{n}", [P, H]) for n in range(2)]
        xt = [sb(f"xt{n}", [P, H]) for n in range(2)]
        h1 = sb("h1", [P, M])
        h2 = sb("h2", [P, M])
        h1T = [sb(f"h1T{n}", [P, M]) for n in range(2)]
        h2T = [sb(f"h2T{n}", [P, M]) for n in range(2)]
        y = [sb(f"y{n}", [P, H]) for n in range(2)]

        b1_b = sb("b1_b", [P, E * M])
        b2_b = sb("b2_b", [P, E * M])
        b3_b = sb("b3_b", [P, E * H])
        ident = sb("ident", [P, P])
        ident16 = sb("ident16", [P, P], BF16)
        ones16 = rows[0][:, 0:P // 2].bitcast(BF16)
        ones32 = sb("ones32", [P, P])
        earlier = rows[1][:, 0:P // 2].bitcast(BF16)
        count_r = tmp(P)
        count_t = tmp(NT)
        count_e = y[1][:, 3 * E:4 * E]
        col_no = y[1][:, P:P + C]
        part_no = sb("part_no", [P, 1])
        full_at = h2T[1][:, 8 * C:9 * C]
        dummy_no = tmp(NT)
        batch_half = h1T[0][0:NB, 0:P]
        batch_col = xt[1][0:NB, P // 2:P // 2 + C]
        rms_sb = y[0][:, 0:HK]
        wg_sb = xt[1][:, 0:HK * E].rearrange("p (k e) -> p k e", k=HK)
        wgf = xt[1][:, HK * E:2 * HK * E].rearrange("p (k e) -> p k e", k=HK)
        condT_sb = xt[1][0:G, P:P + NB]
        gg_sb = y[0][0:G, 1 * E:2 * E]
        wgb_sb = y[0][0:NB, 2 * E:3 * E]
        ggb_sb = y[0][0:NB, 3 * E:4 * E]
        gb = y[0][0:NB, 4 * E:5 * E]
        gb_col = h1T[1][0:NB, 0:CW]
        sumsq = h2T[1][:, 0 * C:1 * C]
        mean_sq = h2T[1][:, 1 * C:2 * C]
        root = h2T[1][:, 2 * C:3 * C]
        rs = h2T[1][:, 3 * C:4 * C]
        tmp_c = h2T[1][:, 4 * C:5 * C]
        zero = sb("zero", [P, 1])
        prob = tmp(CW)
        rest = tmp(CW)
        t8 = tmp(CW)
        is_first = tmp(CW)
        is_second = tmp(CW)
        chosen16 = tmp(CW // 2).bitcast(BF16)
        top = h2T[1][:, 5 * C:6 * C]
        first = h2T[1][:, 6 * C:7 * C]
        second = h2T[1][:, 7 * C:8 * C]
        which = sb("which", [P, 2, C])
        pair_w = sb("pair_w", [P, 2, C])
        tot = tmp(CW)
        seg = tmp(CW)
        incl = tmp(CW)
        n_over = tmp(E * C)
        n_tiles = y[1][:, 0 * E:1 * E]
        tile_end = y[1][:, 1 * E:2 * E]
        one_e = y[1][:, 2 * E:3 * E]
        slot_at = tmp(CW)
        slot = h2T[0][:, 0 * C:2 * C].rearrange("p (k c) -> p k c", k=2)
        slot_i = h2T[0][:, 6 * C:8 * C].bitcast(I32).rearrange("p (k c) -> p k c", k=2)
        slot_hi = h2T[0][:, 8 * C:10 * C].bitcast(I32).rearrange("p (k c) -> p k c", k=2)
        slot_lo = h2T[0][:, 10 * C:12 * C].bitcast(I32).rearrange("p (k c) -> p k c", k=2)
        slot_t = h2T[0][:, 2 * C:4 * C].rearrange("p (k c) -> p k c", k=2)
        slot_r = h2T[0][:, 4 * C:6 * C].rearrange("p (k c) -> p k c", k=2)
        past = tmp(NT * (E - 1))
        tile_e = sb("tile_e", [P, NT], I32)
        low_done_f = sb("low_done_f", [P, 1])
        low_done_i = sb("low_done_i", [P, 1], I32)
        low_done = sb("low_done", [P, 1], I32)
        tab = tmp(2 * NT)
        tab_k = tmp(NT)
        tab_v = tmp(NT)
        tab_x = tmp(NT)
        take_row = sb("take_row", [P, NT], I32)
        put_row = sb("put_row", [P, NT], I32)

        fw_sb = h1
        fw_pos = h2
        fw_q = sb("fw_q", [P, HK, H], BF16)
        fb_b = sb("fb_b", [P, H])
        fsum = sb("fsum", [P, 1])
        w_scale = sb("w_scale", [P, 1])
        thr = sb("thr", [P, 2])
        amax = sb("amax", [P, 4])
        amax1 = sb("amax1", [P, 1])
        amax_row = sb("amax_row", [1, 1])
        i_scale = sb("i_scale", [P, 1])
        i_inv = sb("i_inv", [P, 1])
        out_scale = sb("out_scale", [P, 1])
        magic = sb("magic", [P, 1])

        bank = [ctx.enter_context(nc.psum_tensor(f"bank{n}", [P, 512], F32)) for n in range(8)]
        p_l1, p_l2, p_l3, p_t0, p_t1, p_t2 = bank[:6]
        p_rank, p_total, p_table = bank[0], bank[1], bank[2]
        p_gate, p_small = bank[6], bank[7]
        p_qT = [bank[0], bank[1]]
        p_out = [[bank[2], bank[3]], [bank[4], bank[5]]]

        small_in = sem("small_in")
        ffn_in = sem("ffn_in")
        bias_in = sem("bias_in")
        feat_in = [sem(f"feat_in{n}") for n in range(4)]
        tok_in = [sem(f"tok_in{n}") for n in range(4)]
        w_in = [sem(f"w_in{n}") for n in range(E)]
        weights_ready = sem("weights_ready")
        pool_step = sem("pool_step")
        consts_ready = sem("consts_ready")
        vec_step = sem("vec_step")
        quant_step = sem("quant_step")
        wgf_ready = sem("wgf_ready")
        cond_done = sem("cond_done")
        gb_ready = sem("gb_ready")
        gates_done = sem("gates_done")
        sumsq_done = sem("sumsq_done")
        mean_ready = sem("mean_ready")
        root_ready = sem("root_ready")
        logits_ready = sem("logits_ready")
        exp_done = sem("exp_done")
        chosen_ready = sem("chosen_ready")
        ranks_done = sem("ranks_done")
        onehots_ready = sem("onehots_ready")
        onehots_p = sem("onehots_p")
        tables_done = sem("tables_done")
        routed = sem("routed")
        fsum_ready = sem("fsum_ready")
        fsum_done = sem("fsum_done")
        dma_go = sem("dma_go")
        take_set = sem("take_set")
        put_set = sem("put_set")
        gathered = [sem(f"gathered{n}") for n in range(2)]
        scattered = [sem(f"scattered{n}") for n in range(2)]
        t0_done, xt_ready = sem("t0_done"), sem("xt_ready")
        l1_done, h1_ready, t1_done, h1T_ready = sem("l1_done"), sem("h1_ready"), sem("t1_done"), sem("h1T_ready")
        l2_done, h2_ready, t2_done, h2T_ready = sem("l2_done"), sem("h2_ready"), sem("t2_done"), sem("h2T_ready")
        l3_done, y_ready = sem("l3_done"), sem("y_ready")
        low_in = [sem(f"low_in{n}") for n in range(4)]
        high_in = [sem(f"high_in{n}") for n in range(4)]
        res_in = sem("res_in")
        low_scaled = sem("low_scaled")
        res_biased = sem("res_biased")
        amax_ready, amax_T, amax_one, amax_all, scales_ready = (
            sem("amax_ready"), sem("amax_T"), sem("amax_one"), sem("amax_all"), sem("scales_ready"))
        rounded, q_ready, qT_done, qT_ready, ffn_done, res_ready = (
            sem("rounded"), sem("q_ready"), sem("qT_done"), sem("qT_ready"), sem("ffn_done"), sem("res_ready"))
        stored = [sem(f"stored{n}") for n in range(2)]

        PEEL, TURNS = 6, NT + 3
        STEADY = (NT - 3 - PEEL) // 2 * 2

        def turns(eng, body):
            for i in range(PEEL):
                body(0, i)
            with eng.Fori(0, STEADY // 2) as pair:
                body(pair, PEEL)
                body(pair, PEEL + 1)
            for i in range(PEEL + STEADY, TURNS):
                body(0, i)

        def is_tile(pair, n):
            return not isinstance(pair, int) or 0 <= n < NT

        def later(pair, n, first):
            return not isinstance(pair, int) or n >= first

        def groups(eng, body):
            body(0, 0)
            body(0, 1)
            with eng.Fori(0, NG // 2 - 1) as pair:
                body(pair, 2)
                body(pair, 3)

        block = ctx.enter_context(nc.Block())
        QC = C // 4

        def quarter(ap, n):
            return ap[:, n * QC * H:(n + 1) * QC * H].rearrange("p (c h) -> p c h", c=QC)

        def token_rows(dram, first_row, n):
            return dram[first_row + n * QC * P:first_row + (n + 1) * QC * P, :].rearrange("(c p) h -> p c h", p=P)

        @block.sync
        def _(sp):
            for n in range(4):
                sp.dma_start(x_feat[:, :, n * QC * P:(n + 1) * QC * P],
                             xT[:, n * QC * P:(n + 1) * QC * P].rearrange("(k p) t -> p k t", p=P)
                             ).then_inc(feat_in[n], 16)
                sp.dma_start(quarter(x_tok, n), token_rows(x, 0, n)).then_inc(tok_in[n], 16)
            for e in range(4):
                sp.dma_start(area(e, WE), w[:, e, :]).then_inc(w_in[e], 16)
            for e in range(4):
                sp.wait_ge(w_in[e], 16)
                sp.sem_inc(weights_ready, 1)
            sp.wait_ge(routed, 1)
            for e in range(4, E):
                sp.dma_start(area(e, WE), w[:, e, :]).then_inc(w_in[e], 16)
            for e in range(4, E):
                sp.wait_ge(w_in[e], 16)
                sp.sem_inc(weights_ready, 1)
            low_rows = sp.value_load(low_done[0:1, 0:1], min_val=0, max_val=16 * NT)
            sp.wait_ge(scattered[0], low_rows)
            sp.wait_ge(scattered[1], low_rows)
            for n in range(4):
                sp.dma_start(quarter(y_low, n), token_rows(pair_rows, 0, n)).then_inc(low_in[n], 16)
            sp.dma_start(x_res.rearrange("p (c h) -> p c h", c=C), x.rearrange("(c p) h -> p c h", p=P)).then_inc(res_in, 16)
            sp.wait_ge(scattered[0], 16 * ((NT + 1) // 2))
            sp.wait_ge(scattered[1], 16 * (NT // 2))
            for n in range(4):
                sp.dma_start(quarter(y_high, n), token_rows(pair_rows, T, n)).then_inc(high_in[n], 16)
            out_v = out.rearrange("(g c p) h -> p g c h", p=P, c=CG)
            with sp.Fori(0, NG // 2) as turn:
                for n in range(2):
                    sp.wait_ge(res_ready, 2 * turn + n + 1)
                    sp.dma_start(out_v[:, bass.ds(2 * turn + n, 1), :, :].rearrange("p g c h -> p (g c) h"),
                                 res[n][:, :].rearrange("p (c h) -> p c h", c=CG)).then_inc(stored[n], 16)
            for n in range(2):
                sp.wait_ge(stored[n], 16 * (NG // 2))

        @block.gpsimd
        def _(pool):
            steps = [0]

            def step(ins):
                steps[0] += 1
                ins.then_inc(pool_step, 1)
                pool.wait_ge(pool_step, steps[0])

            for dst, value in ((ident, 0.0), (ident16, 0.0), (earlier, 1.0), (batch_half, 0.0), (batch_col, 0.0),
                               (ones16, 1.0), (ones32, 1.0)):
                step(nc.gpsimd.memset(dst[:, :], value))
            for m in (ident, ident16):
                step(nc.gpsimd.affine_select(out=m[:, :], in_=m[:, :], compare_op=ALU.not_equal, fill=1.0, base=0,
                                             pattern=[[-1, P]], channel_multiplier=1))
            step(nc.gpsimd.affine_select(out=earlier[:, :], in_=earlier[:, :], compare_op=ALU.is_gt, fill=0.0, base=0,
                                         pattern=[[1, P]], channel_multiplier=-1))
            step(nc.gpsimd.memset(batch_half[0:C, 0:SB], 1.0))
            step(nc.gpsimd.memset(batch_half[C:2 * C, SB:P], 1.0))
            for h in range(2):
                step(nc.gpsimd.affine_select(out=batch_col[:, :], in_=batch_col[:, :], compare_op=ALU.not_equal,
                                             fill=1.0, base=-h * C, pattern=[[-1, C]], channel_multiplier=1))

            def count(out_ap, pattern, base=0, mult=0):
                return nc.gpsimd.iota(out_ap, pattern=pattern, base=base, channel_multiplier=mult,
                                      allow_small_or_imprecise_dtypes=True)

            step(count(count_r[:, :], [[1, P]]))
            step(count(count_t[:, :], [[1, NT]]))
            step(count(count_e[:, :], [[1, E]]))
            step(count(col_no[:, :], [[1, C]], base=1))
            step(count(part_no[:, :], [[0, 1]], mult=1))
            step(count(full_at[:, :], [[P, C]]))
            step(count(dummy_no[:, 0:NT - 1].rearrange("p (a b) -> p a b", b=2), [[0, NT // 2], [P, 2]],
                       base=DUMMY + P, mult=1))
            step(count(dummy_no[:, NT - 1:NT], [[0, 1]], base=DUMMY + P, mult=1))
            pool.sem_inc(consts_ready, 1)

            pool.wait_ge(routed, 1)

            def gather(pair, n):
                i, b = 2 * pair + n, n % 2
                if later(pair, n, 2):
                    pool.wait_ge(t0_done, i - 1)
                nc.gpsimd.tensor_copy(take_now[b][:, :], take_row[:, bass.ds(i, 1)]).then_inc(take_set, 1)
                pool.wait_ge(take_set, i + 1)
                pool.sem_inc(dma_go, 1)
                nc.gpsimd.indirect_dma_start(
                    rows[b][:, :], None, x, bass.IndirectOffsetOnAxis(ap=take_now[b][:, 0:1].bitcast(U32), axis=0)
                ).then_inc(gathered[b], 16)

            def scatter(pair, n):
                i, b = 2 * pair + n, n % 2
                if later(pair, n, 2):
                    pool.wait_ge(scattered[b], 16 * (pair + n // 2))
                nc.gpsimd.tensor_copy(put_now[b][:, :], put_row[:, bass.ds(i, 1)]).then_inc(put_set, 1)
                pool.wait_ge(put_set, i + 1)
                pool.wait_ge(y_ready, i + 1)
                pool.sem_inc(dma_go, 1)
                nc.gpsimd.indirect_dma_start(
                    pair_rows, bass.IndirectOffsetOnAxis(ap=put_now[b][:, 0:1].bitcast(U32), axis=0), y[b][:, :], None
                ).then_inc(scattered[b], 16)

            for i in range(3):
                gather(0, i)

            def turn(pair, n):
                if is_tile(pair, n + 3):
                    gather(pair, n + 3)
                if is_tile(pair, n - 3):
                    scatter(pair, n - 3)

            turns(pool, turn)

            pool.wait_ge(res_in, 16)
            pool.wait_ge(ffn_in, 32)
            xr = x_res.rearrange("p (c h) -> p c h", c=C)
            for n in range(4):
                part = xr[:, n * QC:(n + 1) * QC, :]
                nc.gpsimd.tensor_tensor(part, part, fb_b[:, :].unsqueeze(1).to_broadcast([P, QC, H]),
                                        ALU.add).then_inc(res_biased, 1)

        @block.scalar
        def _(act):
            for dst, src in ((rms_sb[:, :], rms), (wg_sb[:, :, :], wg.rearrange("(k p) e -> p k e", p=P)),
                             (condT_sb[:, :], condT), (gg_sb[:, :], gg), (wgb_sb[:, :], wgb.partition_broadcast(NB)),
                             (ggb_sb[:, :], ggb.partition_broadcast(NB))):
                act.dma_start(dst, src).then_inc(small_in, 16)
            act.dma_start(fw_sb[:, :].rearrange("p (k o) -> p k o", k=HK),
                          fwT.rearrange("(k p) o -> p k o", p=P)).then_inc(ffn_in, 16)
            act.dma_start(fb_b[:, :], fbias.partition_broadcast(P)).then_inc(ffn_in, 16)
            for dst, src in ((b1_b, b1), (b2_b, b2), (b3_b, b3)):
                act.dma_start(dst[:, :], src.rearrange("e m -> (e m)").partition_broadcast(P)).then_inc(bias_in, 16)
            for n in range(4):
                act.wait_ge(tok_in[n], 16)
                for c in range(n * QC, (n + 1) * QC):
                    part = x_tok[:, c * H:(c + 1) * H]
                    last = nc.scalar.activation(part, part, ACT.Square, accum_out=sumsq[:, c:c + 1])
            last.then_inc(sumsq_done, 1)
            act.wait_ge(mean_ready, 1)
            nc.scalar.activation(root[:, :], mean_sq[:, :], ACT.Sqrt).then_inc(root_ready, 1)
            act.wait_ge(logits_ready, 1)
            nc.scalar.activation(prob[:, :], rest[:, :], ACT.Exp).then_inc(exp_done, 1)
            for k in range(2):
                act.wait_ge(onehots_ready, k + 1)
                nc.scalar.activation(onehot_t[k][:, :, 1, :], onehot_t[k][:, :, 1, :], ACT.Copy,
                                     scale=part_no[:, 0:1]).then_inc(onehots_p, 1)

            def turn(pair, n):
                i, b = 2 * pair + n, n % 2
                if is_tile(pair, n - 2):
                    act.wait_ge(t2_done, i - 1)
                    if later(pair, n, 4):
                        act.wait_ge(l3_done, i - 3)
                    nc.scalar.activation(h2T[b][:, :], p_t2[:, :], ACT.Relu).then_inc(h2T_ready, 1)
                if is_tile(pair, n + 1):
                    act.wait_ge(t0_done, i + 2)
                    if later(pair, n, 1):
                        act.wait_ge(l1_done, i)
                    nc.scalar.activation(xt[1 - b][:, :], p_t0[:, 0:H], ACT.Copy).then_inc(xt_ready, 1)
                if is_tile(pair, n):
                    act.wait_ge(t1_done, i + 1)
                    if later(pair, n, 2):
                        act.wait_ge(l2_done, i - 1)
                    nc.scalar.activation(h1T[b][:, :], p_t1[:, :], ACT.Relu).then_inc(h1T_ready, 1)

            act.wait_ge(t0_done, 1)
            nc.scalar.activation(xt[0][:, :], p_t0[:, 0:H], ACT.Copy).then_inc(xt_ready, 1)
            turns(act, turn)

            for n in range(4):
                act.wait_ge(low_in[n], 16)
                for c in range(n * QC, (n + 1) * QC):
                    part = y_low[:, c * H:(c + 1) * H]
                    last = nc.scalar.activation(part, part, ACT.Copy, scale=pair_w[:, 0, c:c + 1])
                last.then_inc(low_scaled, 1)

            def group(pair, n):
                g, b = 2 * pair + n, n % 2
                act.wait_ge(rounded, g + 1)
                if later(pair, n, 2):
                    act.wait_ge(qT_done, g - 1)
                nc.scalar.activation(q16[b][:, :], y_high[:, bass.ds(g * CG * H, CG * H)], ACT.Identity,
                                     bias=magic[:, 0:1]).then_inc(q_ready, 1)
                act.wait_ge(qT_done, g + 1)
                if later(pair, n, 2):
                    act.wait_ge(ffn_done, g - 1)
                nc.scalar.activation(qT[b][:, :], p_qT[b][:, :].bitcast(BF16), ACT.Copy).then_inc(qT_ready, 1)

            groups(act, group)

        @block.vector
        def _(dve):
            steps = [0]
            V = nc.vector

            def step(ins):
                steps[0] += 1
                ins.then_inc(vec_step, 1)
                dve.wait_ge(vec_step, steps[0])

            def by_ce(ap):
                return ap.rearrange("p (c e) -> p c e", e=E)

            def over_e(ap):
                return ap.unsqueeze(2).to_broadcast([P, C, E])

            e_of = count_e[:, :].unsqueeze(1).to_broadcast([P, C, E])

            step(V.memset(magic[:, :], -MAGIC))
            step(V.memset(one_e[:, :], 1.0))
            step(V.memset(seg[:, :], 1.0))
            step(V.memset(seg[:, :].rearrange("p (e c) -> p e c", e=E)[:, :, 0:1], 0.0))
            dve.wait_ge(small_in, 16 * 6)
            for k in range(HK):
                step(V.tensor_scalar(wgf[:, k, :], wg_sb[:, k, :], rms_sb[:, k:k + 1], None, ALU.mult))
            V.memset(zero[:, :], 0.0).then_inc(wgf_ready, 1)
            dve.wait_ge(cond_done, 1)
            dve.wait_ge(consts_ready, 1)
            step(V.tensor_tensor(gb[:, :], p_small[0:NB, 0:E], wgb_sb[:, :], ALU.add))
            step(V.tensor_tensor(gb[:, :], gb[:, :], ggb_sb[:, :], ALU.add))
            V.tensor_tensor(gb_col[:, :].rearrange("p (c e) -> p c e", e=E),
                            gb[:, :].unsqueeze(1).to_broadcast([NB, C, E]),
                            batch_col[:, :].unsqueeze(2).to_broadcast([NB, C, E]), ALU.mult).then_inc(gb_ready, 1)
            dve.wait_ge(ffn_in, 32)
            V.tensor_reduce(fsum[:, :], fw_sb[:, :], AX.X, ALU.add, apply_absolute_value=True).then_inc(fsum_ready, 1)
            dve.wait_ge(fsum_done, 1)
            step(V.tensor_scalar(w_scale[:, :], p_small[:, 16:17], 1.0 / (H * H), None, ALU.mult))
            step(V.tensor_scalar(thr[:, 0:1], w_scale[:, :], 0.5, None, ALU.mult))
            step(V.tensor_scalar(thr[:, 1:2], w_scale[:, :], -0.5, None, ALU.mult))
            step(V.tensor_scalar(fw_pos[:, :], fw_sb[:, :], thr[:, 0:1], None, ALU.is_gt))
            step(V.scalar_tensor_tensor(fw_pos[:, :], fw_sb[:, :], thr[:, 1:2], fw_pos[:, :], ALU.is_lt, ALU.subtract))
            step(V.tensor_scalar(fw_q[:, :, :].rearrange("p k o -> p (k o)"), fw_pos[:, :], -1.0, None, ALU.mult))

            dve.wait_ge(sumsq_done, 1)
            V.tensor_scalar(mean_sq[:, :], sumsq[:, :], 1.0 / H, 1e-6, ALU.mult, ALU.add).then_inc(mean_ready, 1)
            dve.wait_ge(root_ready, 1)
            step(V.reciprocal(rs[:, :], root[:, :]))
            step(V.tensor_tensor(tmp_c[:, :], rs[:, :], rs[:, :], ALU.mult))
            step(V.tensor_tensor(tmp_c[:, :], tmp_c[:, :], mean_sq[:, :], ALU.mult))
            step(V.tensor_scalar(tmp_c[:, :], tmp_c[:, :], -0.5, 1.5, ALU.mult, ALU.add))
            step(V.tensor_tensor(rs[:, :], rs[:, :], tmp_c[:, :], ALU.mult))

            dve.wait_ge(gates_done, 1)
            step(V.tensor_tensor(by_ce(rest[:, :]), by_ce(p_gate[:, 0:CW]), over_e(rs[:, :]), ALU.mult))
            step(V.tensor_tensor(rest[:, :], rest[:, :], p_gate[:, CW:2 * CW], ALU.add))
            step(V.tensor_reduce(top[:, :], by_ce(rest[:, :]), AX.X, ALU.max))
            V.tensor_tensor(by_ce(rest[:, :]), by_ce(rest[:, :]), over_e(top[:, :]), ALU.subtract).then_inc(logits_ready, 1)
            dve.wait_ge(exp_done, 1)
            step(V.tensor_reduce(top[:, :], by_ce(prob[:, :]), AX.X, ALU.add))
            step(V.reciprocal(top[:, :], top[:, :]))
            step(V.tensor_tensor(by_ce(prob[:, :]), by_ce(prob[:, :]), over_e(top[:, :]), ALU.mult))

            def largest(values, number, onehot):
                step(V.tensor_reduce(top[:, :], by_ce(values[:, :]), AX.X, ALU.max))
                step(V.tensor_tensor(by_ce(t8[:, :]), by_ce(values[:, :]), over_e(top[:, :]), ALU.is_equal))
                step(V.scalar_tensor_tensor(by_ce(t8[:, :]), by_ce(t8[:, :]), -float(E), e_of, ALU.mult, ALU.add))
                step(V.tensor_reduce(number[:, :], by_ce(t8[:, :]), AX.X, ALU.min))
                step(V.tensor_scalar(number[:, :], number[:, :], float(E), None, ALU.add))
                step(V.tensor_tensor(by_ce(onehot[:, :]), e_of, over_e(number[:, :]), ALU.is_equal))

            largest(prob, first, is_first)
            step(V.scalar_tensor_tensor(rest[:, :], is_first[:, :], -2.0, prob[:, :], ALU.mult, ALU.add))
            largest(rest, second, is_second)
            V.tensor_tensor(chosen16[:, :], is_first[:, :], is_second[:, :], ALU.add).then_inc(chosen_ready, 1)
            step(V.tensor_tensor(which[:, 0, :], first[:, :], second[:, :], ALU.min))
            step(V.tensor_tensor(which[:, 1, :], first[:, :], second[:, :], ALU.max))
            step(V.tensor_tensor(by_ce(is_first[:, :]), e_of, over_e(which[:, 0, :]), ALU.is_equal))
            step(V.tensor_tensor(by_ce(is_second[:, :]), e_of, over_e(which[:, 1, :]), ALU.is_equal))

            def pick(dst, onehot, values):
                step(V.tensor_tensor(t8[:, :], onehot[:, :], values[:, :], ALU.mult))
                step(V.tensor_reduce(dst, by_ce(t8[:, :]), AX.X, ALU.add))

            pick(pair_w[:, 0, :], is_first, prob)
            pick(pair_w[:, 1, :], is_second, prob)

            dve.wait_ge(ranks_done, 1)
            step(V.tensor_copy(tot[:, :].rearrange("p (e c) -> p e c", e=E),
                               p_total[:, 0:CW].rearrange("p (c e) -> p e c", e=E)))
            step(V.tensor_tensor_scan(incl[:, :], seg[:, :], tot[:, :], 0.0, ALU.mult, ALU.add))
            in_expert = incl[:, :].rearrange("p (e c) -> p e c", e=E)
            step(V.tensor_tensor(n_over[:, :].rearrange("p (e c) -> p e c", e=E),
                                 in_expert[:, :, C - 1:C].to_broadcast([P, E, C]),
                                 full_at[:, :].unsqueeze(1).to_broadcast([P, E, C]), ALU.is_gt))
            step(V.tensor_reduce(n_tiles[:, :], n_over[:, :].rearrange("p (e c) -> p e c", e=E), AX.X, ALU.add))
            step(V.tensor_scalar(n_tiles[:, :], n_tiles[:, :], 1.0, None, ALU.max))
            step(V.tensor_tensor_scan(tile_end[:, :], one_e[:, :], n_tiles[:, :], 0.0, ALU.mult, ALU.add))
            step(V.tensor_tensor(n_tiles[:, :], tile_end[:, :], n_tiles[:, :], ALU.subtract))
            step(V.tensor_tensor(tot[:, :], incl[:, :], tot[:, :], ALU.subtract))
            step(V.tensor_tensor(by_ce(slot_at[:, :]), by_ce(p_rank[:, 0:CW]),
                                 tot[:, :].rearrange("p (e c) -> p c e", e=E), ALU.add))
            step(V.scalar_tensor_tensor(by_ce(slot_at[:, :]), n_tiles[:, :].unsqueeze(1).to_broadcast([P, C, E]),
                                        float(P), by_ce(slot_at[:, :]), ALU.mult, ALU.add))
            pick(slot[:, 0, :], is_first, slot_at)
            pick(slot[:, 1, :], is_second, slot_at)
            step(V.tensor_copy(slot_i[:, :, :], slot[:, :, :]))
            step(V.tensor_scalar(slot_hi[:, :, :], slot_i[:, :, :], 7, None, ALU.arith_shift_right))
            step(V.tensor_scalar(slot_lo[:, :, :], slot_i[:, :, :], P - 1, None, ALU.bitwise_and))
            step(V.tensor_copy(slot_t[:, :, :], slot_hi[:, :, :]))
            step(V.tensor_copy(slot_r[:, :, :], slot_lo[:, :, :]))

            for k in range(2):
                step(V.tensor_tensor(onehot_t[k][:, :, 1, :], slot_t[:, k, :].unsqueeze(2).to_broadcast([P, C, NT]),
                                     count_t[:, :].unsqueeze(1).to_broadcast([P, C, NT]), ALU.is_equal))
                step(V.tensor_tensor(onehot_t[k][:, :, 0, :], onehot_t[k][:, :, 1, :],
                                     col_no[:, :].unsqueeze(2).to_broadcast([P, C, NT]), ALU.mult))
                V.tensor_tensor(onehot_r[k][:, :, :], slot_r[:, k, :].unsqueeze(2).to_broadcast([P, C, P]),
                                count_r[:, :].unsqueeze(1).to_broadcast([P, C, P]), ALU.is_equal).then_inc(onehots_ready, 1)
                if k == 0:
                    step(V.tensor_scalar(col_no[:, :], col_no[:, :], float(C), None, ALU.add))

            step(V.tensor_tensor(past[:, :].rearrange("p (t e) -> p t e", t=NT),
                                 count_t[:, :].unsqueeze(2).to_broadcast([P, NT, E - 1]),
                                 tile_end[:, 0:E - 1].unsqueeze(1).to_broadcast([P, NT, E - 1]), ALU.is_ge))
            step(V.tensor_reduce(tab_x[:, :], past[:, :].rearrange("p (t e) -> p t e", t=NT), AX.X, ALU.add))
            step(V.tensor_copy(tile_e[:, :], tab_x[:, :]))
            step(V.tensor_scalar(low_done_f[:, :], n_tiles[:, E - 1:E], 8.0, 8.0, ALU.mult, ALU.add))
            step(V.tensor_copy(low_done_i[:, :], low_done_f[:, :]))
            step(V.tensor_scalar(low_done[:, :], low_done_i[:, :], -16, None, ALU.bitwise_and))

            dve.wait_ge(tables_done, 1)
            step(V.tensor_copy(tab[:, :], p_table[:, 0:2 * NT]))
            a, b_ = tab[:, 0:NT], tab[:, NT:2 * NT]
            step(V.scalar_tensor_tensor(tab_x[:, :], a, float(P), b_, ALU.mult, ALU.add))
            step(V.tensor_scalar(tab_k[:, :], a, C + 0.5, None, ALU.is_gt))
            step(V.scalar_tensor_tensor(tab_k[:, :], tab_k[:, :], -float(T), tab_x[:, :], ALU.mult, ALU.add))
            step(V.tensor_scalar(take_row[:, :], tab_k[:, :], -float(P), 0.0, ALU.add, ALU.max))
            step(V.tensor_scalar(tab_v[:, :], a, 0.5, None, ALU.is_lt))
            step(V.tensor_tensor(tab_v[:, :], tab_v[:, :], dummy_no[:, :], ALU.mult))
            step(V.tensor_tensor(tab_x[:, :], tab_x[:, :], tab_v[:, :], ALU.add))
            V.tensor_scalar(put_row[:, :], tab_x[:, :], -float(P), None, ALU.add).then_inc(routed, 1)

            dve.wait_ge(routed, 1)
            dve.wait_ge(bias_in, 48)

            def expert(pair, n):
                return dve.value_load(tile_e[0:1, bass.ds(2 * pair + n, 1)], min_val=0, max_val=E - 1)

            def turn(pair, n):
                i, b = 2 * pair + n, n % 2
                if is_tile(pair, n):
                    e = expert(pair, n)
                    dve.wait_ge(l1_done, i + 1)
                    if later(pair, n, 1):
                        dve.wait_ge(t1_done, i)
                    V.tensor_tensor(h1[:, :], p_l1[:, :], b1_b[:, bass.ds(e * M, M)],
                                    ALU.add).then_inc(h1_ready, 1)
                if is_tile(pair, n - 3):
                    e = expert(pair, n - 3)
                    dve.wait_ge(l3_done, i - 2)
                    if later(pair, n, 5):
                        dve.wait_ge(scattered[1 - b], 16 * (pair + (n - 3) // 2))
                    V.tensor_tensor(y[1 - b][:, :], p_l3[:, 0:H], b3_b[:, bass.ds(e * H, H)],
                                    ALU.add).then_inc(y_ready, 1)
                if is_tile(pair, n - 1):
                    e = expert(pair, n - 1)
                    dve.wait_ge(l2_done, i)
                    if later(pair, n, 2):
                        dve.wait_ge(t2_done, i - 1)
                    V.tensor_tensor(h2[:, :], p_l2[:, :], b2_b[:, bass.ds(e * M, M)],
                                    ALU.add).then_inc(h2_ready, 1)

            turns(dve, turn)

            for n in range(4):
                dve.wait_ge(high_in[n], 16)
                dve.wait_ge(low_scaled, n + 1)
                for c in range(n * QC, (n + 1) * QC):
                    part = y_high[:, c * H:(c + 1) * H]
                    last = V.scalar_tensor_tensor(part, part, pair_w[:, 1, c:c + 1], y_low[:, c * H:(c + 1) * H],
                                                  ALU.mult, ALU.add)
                step(last)
                step(V.tensor_reduce(amax[:, n:n + 1], y_high[:, n * QC * H:(n + 1) * QC * H], AX.X, ALU.max,
                                     apply_absolute_value=True))
            V.tensor_reduce(amax1[:, :], amax[:, :], AX.X, ALU.max).then_inc(amax_ready, 1)
            dve.wait_ge(amax_T, 1)
            V.tensor_reduce(amax_row[:, :], p_small[0:1, 0:P], AX.X, ALU.max).then_inc(amax_one, 1)
            dve.wait_ge(amax_all, 1)
            step(V.tensor_scalar(i_scale[:, :], p_small[:, 0:1], 1.0 / 127.0, None, ALU.mult))
            step(V.reciprocal(i_inv[:, :], i_scale[:, :]))
            step(V.tensor_tensor(out_scale[:, :], w_scale[:, :], i_scale[:, :], ALU.mult))

            def quantize(pair, n):
                g = 2 * pair + n
                part = y_high[:, bass.ds(g * CG * H, CG * H)]
                step_q(V.tensor_scalar(part, part, i_inv[:, 0:1], MAGIC, ALU.mult, ALU.add), 2 * pair + n + 1)
                V.tensor_scalar(part, part, MAGIC - 128.0, MAGIC + 127.0, ALU.max, ALU.min).then_inc(rounded, 1)

            def step_q(ins, n):
                ins.then_inc(quant_step, 1)
                dve.wait_ge(quant_step, n)

            def finish(pair, n):
                g = 2 * pair + n
                dve.wait_ge(ffn_done, g + 1)
                if later(pair, n, 2):
                    dve.wait_ge(stored[n % 2], 16 * (pair + n // 2))
                for h in range(2):
                    last = V.scalar_tensor_tensor(
                        res[n % 2][:, h * 2 * H:(h + 1) * 2 * H], p_out[n % 2][h][:, :], out_scale[:, 0:1],
                        x_res[:, bass.ds(g * CG * H + h * 2 * H, 2 * H)], ALU.mult, ALU.add)
                last.then_inc(res_ready, 1)

            quantize(0, 0)
            quantize(0, 1)
            dve.wait_ge(res_biased, 4)

            finish(0, 0)
            quantize(0, 2)
            finish(0, 1)
            quantize(0, 3)
            with dve.Fori(0, NG // 2 - 2) as pair:
                for n in (2, 3):
                    finish(pair, n)
                    quantize(pair, n + 2)
            for n in range(NG - 2, NG):
                finish(0, n)

        @block.tensor
        def _(pe):
            PE = nc.tensor
            pe.wait_ge(small_in, 16 * 6)
            PE.matmul(p_small[0:NB, 0:E], condT_sb[:, :], gg_sb[:, :], start=True, stop=True).then_inc(cond_done, 1)
            pe.wait_ge(wgf_ready, 1)
            for n in range(4):
                pe.wait_ge(feat_in[n], 16)
                for c in range(n * QC, (n + 1) * QC):
                    for k in range(HK):
                        PE.matmul(p_gate[:, c * E:(c + 1) * E], x_feat[:, k, c * P:(c + 1) * P], wgf[:, k, :],
                                  start=(k == 0), stop=(k == HK - 1))
            pe.wait_ge(gb_ready, 1)
            PE.matmul(p_gate[:, CW:2 * CW], batch_half[:, :], gb_col[:, :], start=True, stop=True).then_inc(gates_done, 1)
            pe.wait_ge(fsum_ready, 1)
            PE.matmul(p_small[:, 16:17], ones32[:, :], fsum[:, :], start=True, stop=True).then_inc(fsum_done, 1)
            pe.wait_ge(chosen_ready, 1)
            PE.matmul(p_rank[:, 0:CW], earlier[:, :], chosen16[:, :], start=True, stop=True)
            PE.matmul(p_total[:, 0:CW], ones16[:, :], chosen16[:, :], start=True, stop=True).then_inc(ranks_done, 1)
            for k in range(2):
                pe.wait_ge(onehots_ready, k + 1)
                pe.wait_ge(onehots_p, k + 1)
                for c in range(C):
                    last = PE.matmul(p_table[:, 0:2 * NT], onehot_r[k][:, c, :],
                                     onehot_t[k][:, c, :, :].rearrange("p v t -> p (v t)"),
                                     start=(k == 0 and c == 0), stop=(k == 1 and c == C - 1))
            last.then_inc(tables_done, 1)

            pe.wait_ge(routed, 1)

            def expert(pair, n):
                return pe.value_load(tile_e[0:1, bass.ds(2 * pair + n, 1)], min_val=0, max_val=E - 1)

            def product(psum, lhs, chunks, width, e, offset, done):
                for k in range(chunks):
                    last = PE.matmul(psum[:, 0:width], lhs[:, k * P:(k + 1) * P],
                                     arena[:, bass.ds(e * WE + (offset + k * width), width)],
                                     start=(k == 0), stop=(k == chunks - 1))
                last.then_inc(done, 1)

            def transposes(psum, src, chunks, done):
                for k in range(chunks):
                    last = PE.transpose(psum[:, k * P:(k + 1) * P], src[:, k * P:(k + 1) * P], ident[:, :])
                last.then_inc(done, 1)

            def transpose_rows(pair, n):
                pe.wait_ge(gathered[n % 2], 16 * (pair + n // 2 + 1))
                if later(pair, n, 1):
                    pe.wait_ge(xt_ready, 2 * pair + n)
                transposes(p_t0, rows[n % 2], HK, t0_done)

            def turn(pair, n):
                i, b = 2 * pair + n, n % 2
                if is_tile(pair, n):
                    e = expert(pair, n)
                    pe.wait_ge(weights_ready, e + 1)
                    pe.wait_ge(xt_ready, i + 1)
                    if later(pair, n, 1):
                        pe.wait_ge(h1_ready, i)
                    product(p_l1, xt[b], HK, M, e, 0, l1_done)
                if is_tile(pair, n - 2):
                    pe.wait_ge(h2_ready, i - 1)
                    if later(pair, n, 3):
                        pe.wait_ge(h2T_ready, i - 2)
                    transposes(p_t2, h2, MK, t2_done)
                if is_tile(pair, n + 1):
                    transpose_rows(pair, n + 1)
                if is_tile(pair, n - 3):
                    e3 = expert(pair, n - 3)
                    pe.wait_ge(h2T_ready, i - 2)
                    if later(pair, n, 4):
                        pe.wait_ge(y_ready, i - 3)
                    product(p_l3, h2T[1 - b], MK, H, e3, W3O, l3_done)
                if is_tile(pair, n):
                    pe.wait_ge(h1_ready, i + 1)
                    if later(pair, n, 1):
                        pe.wait_ge(h1T_ready, i)
                    transposes(p_t1, h1, MK, t1_done)
                if is_tile(pair, n - 1):
                    e2 = expert(pair, n - 1)
                    pe.wait_ge(h1T_ready, i)
                    if later(pair, n, 2):
                        pe.wait_ge(h2_ready, i - 1)
                    product(p_l2, h1T[1 - b], MK, M, e2, W2O, l2_done)

            transpose_rows(0, 0)
            turns(pe, turn)

            pe.wait_ge(amax_ready, 1)
            PE.transpose(p_small[0:1, 0:P], amax1[:, :], ident[:, :]).then_inc(amax_T, 1)
            pe.wait_ge(amax_one, 1)
            PE.matmul(p_small[:, 0:1], ones32[0:1, :], amax_row[:, :], start=True, stop=True).then_inc(amax_all, 1)

            def group(pair, n):
                g, b = 2 * pair + n, n % 2
                pe.wait_ge(q_ready, g + 1)
                if later(pair, n, 2):
                    pe.wait_ge(qT_ready, g - 1)
                pq = p_qT[b][:, :].bitcast(BF16)
                for j in range(CG * HK):
                    last = PE.transpose(pq[:, j * P:(j + 1) * P], q16[b][:, j * P:(j + 1) * P], ident16[:, :])
                last.then_inc(qT_done, 1)
                pe.wait_ge(qT_ready, g + 1)
                if later(pair, n, 2):
                    pe.wait_ge(res_ready, g - 1)
                for c in range(CG):
                    for k in range(HK):
                        j = c * HK + k
                        last = PE.matmul(p_out[b][c // 2][:, (c % 2) * H:(c % 2 + 1) * H],
                                         qT[b][:, j * P:(j + 1) * P], fw_q[:, k, :],
                                         start=(k == 0), stop=(k == HK - 1))
                last.then_inc(ffn_done, 1)

            groups(pe, group)


def kernel(x, cond_256, L0_cond_rms_w, L0_cond_wg_W, L0_cond_wg_b, L0_cond_gg_W, L0_cond_gg_b, L0_cond_W1,
           L0_cond_b1, L0_cond_W2, L0_cond_b2, L0_cond_W3, L0_cond_b3, L0_ffn_weight, L0_ffn_bias):
    import numpy as np
    import concourse.bacc as bacc
    from concourse.bass_utils import run_bass_kernel_spmd

    def np_(a):
        return np.asarray(a)

    x_rows = np_(x).reshape(-1, np_(x).shape[-1])
    E = np_(L0_cond_W1).shape[0]

    def chunks(a):
        a = np_(a)
        return a.reshape(E, a.shape[1] // 128, 128, a.shape[2]).transpose(2, 0, 1, 3).reshape(128, E, -1)

    arrays = {
        "x": x_rows,
        "xT": x_rows.T,
        "condT": np_(cond_256).reshape(-1, 2, np_(cond_256).shape[-1]).transpose(2, 1, 0).reshape(np_(cond_256).shape[-1], -1),
        "rms": np_(L0_cond_rms_w).reshape(-1, 128).T,
        "wg": np_(L0_cond_wg_W), "wgb": np_(L0_cond_wg_b), "gg": np_(L0_cond_gg_W), "ggb": np_(L0_cond_gg_b),
        "w": np.concatenate([chunks(L0_cond_W1), chunks(L0_cond_W2), chunks(L0_cond_W3)], axis=2),
        "b1": np_(L0_cond_b1), "b2": np_(L0_cond_b2), "b3": np_(L0_cond_b3),
        "fwT": np_(L0_ffn_weight).T, "fbias": np_(L0_ffn_bias),
    }
    arrays = {name: np.ascontiguousarray(a) for name, a in arrays.items()}
    nc = bacc.Bacc("TRN2", target_bir_lowering=False, num_devices=1)
    args = {name: nc.dram_tensor(f"in_{name}", a.shape, mybir.dt.from_np(a.dtype), kind="ExternalInput").ap()
            for name, a in arrays.items()}
    out = nc.dram_tensor("out_0", x_rows.shape, F32, kind="ExternalOutput").ap()
    moe_ffn(nc, out=out, **args)
    r = run_bass_kernel_spmd(nc, [{f"in_{name}": a for name, a in arrays.items()}], core_ids=[0])
    return r.results[0]["out_0"].reshape(np_(x).shape)
```

```python
from contextlib import ExitStack

import concourse.bass as bass
from concourse import mybir

P = 128
ALU = mybir.AluOpType
ACT = mybir.ActivationFunctionType
AX = mybir.AxisListType
F32 = mybir.dt.float32
F32R = mybir.dt.float32r
BF16 = mybir.dt.bfloat16
I32 = mybir.dt.int32
U32 = mybir.dt.uint32
MAGIC = 12582912.0


def moe_ffn(nc, x, xT, condT, rms, wg, wgb, gg, ggb, w, b1, b2, b3, fwT, fbias, out):
    T, H = x.shape
    E = wg.shape[1]
    M = b1.shape[1]
    NB = condT.shape[1]
    G = condT.shape[0]
    C = T // P
    HK, MK = H // P, M // P
    WE = HK * M + MK * M + MK * H
    W2O, W3O = HK * M, HK * M + MK * M
    NT = (2 * T + E * (P - 1)) // P
    NT += NT % 2
    FULL = 2 * T // P // 2
    DUMMY = 2 * T
    CW = C * E
    SB = T // NB
    assert C * 2 == NB and SB * 2 == P and HK == 2 and MK == 4

    with ExitStack() as ctx:
        def sb(name, shape, dt=F32):
            return ctx.enter_context(nc.sbuf_tensor(name, shape, dt))

        def sem(name):
            return ctx.enter_context(nc.semaphore(name))

        pair_rows = nc.dram_tensor("pair_rows", [2 * T + 2 * P, H], F32, kind="Internal").ap()

        CH = 512
        EC = WE // CH
        RING = 3
        SLOT = 2 * WE
        ring_at = (nc.sbuf_base + 31) // 32 * 32
        ring = sb("ring", [P, RING * SLOT], F32R)
        stage = sb("stage", [P, 2 * WE])
        slots = [nc.alloc_sbuf_tensor_at(f"slot{n}", [P, SLOT], F32, offset=ring_at + n * SLOT * 4)
                 for n in range(RING)]

        def slot_words(n, words):
            return slots[n][:, 0:words]

        x_tok = slot_words(1, C * H)
        x_feat = slot_words(2, HK * T).rearrange("p (k t) -> p k t", k=HK)
        half = C * P // 2
        onehot_r, onehot_t, is_in_tile = [], [], []
        for k in range(2):
            onehot_r.append(slots[1 + k][:, 0:half].bitcast(BF16).rearrange("p (c r) -> p c r", c=C))
            onehot_t.append(slots[1 + k][:, half:half + C * NT].bitcast(BF16)
                            .rearrange("p (c v t) -> p c v t", c=C, v=2))
            is_in_tile.append(slots[1 + k][:, half + C * NT:half + C * NT + C * NT // 2].bitcast(BF16)
                              .rearrange("p (c t) -> p c t", c=C))
        y_low = slot_words((E - 2) % RING, C * H)
        x_res = slot_words((E - 3) % RING, C * H)
        y_high = slot_words((E - 1) % RING, C * H)

        CG = 4
        NG = C // CG
        scratch = stage[:, WE:WE + 4 * CG * H]
        q16 = [scratch[:, n * CG * H // 2:(n + 1) * CG * H // 2].bitcast(BF16) for n in range(2)]
        qT = [scratch[:, (n + 2) * CG * H // 2:(n + 3) * CG * H // 2].bitcast(BF16) for n in range(2)]
        res = [scratch[:, (n + 2) * CG * H:(n + 3) * CG * H] for n in range(2)]
        taken = [0]

        def tmp(words):
            taken[0] += words
            assert taken[0] <= scratch.shape[1]
            return scratch[:, taken[0] - words:taken[0]]

        take_now = [sb(f"take_now{n}", [P, 1], I32) for n in range(2)]
        put_now = [sb(f"put_now{n}", [P, 1], I32) for n in range(2)]
        rows = [sb(f"rows{n}", [P, H]) for n in range(2)]
        xt = [sb(f"xt_{n}", [P, H], F32R) for n in ("rounded", "rest")]
        h1 = sb("h1", [P, M])
        h2 = sb("h2", [P, M])
        h1T = [[sb(f"h1T{b}_{n}", [P, M], F32R) for n in ("rounded", "rest")] for b in range(2)]
        h2T = [[sb(f"h2T{b}_{n}", [P, M], F32R) for n in ("rounded", "rest")] for b in range(2)]
        small = sb("small", [P, 21 * C])
        gate_in = sb("gate_in", [P, 2 * P])
        y = [sb(f"y{n}", [P, H]) for n in range(2)]

        b1_b = sb("b1_b", [P, E * M])
        b2_b = sb("b2_b", [P, E * M])
        b3_b = sb("b3_b", [P, E * H])
        ident = sb("ident", [P, P])
        ident16 = sb("ident16", [P, P], BF16)
        ones16 = rows[0][:, 0:P // 2].bitcast(BF16)
        ones32 = sb("ones32", [P, P])
        earlier = rows[1][:, 0:P // 2].bitcast(BF16)
        count_r = tmp(P)
        count_t = tmp(NT)
        count_e = y[1][:, 3 * E:4 * E]
        col_no = y[1][:, P:P + 2 * C]
        part_no = sb("part_no", [P, 1])
        dummy_no = tmp(NT)
        batch_half = rows[0][0:NB, P:2 * P]
        batch_col = gate_in[0:NB, P // 2:P // 2 + C]
        rms_sb = y[0][:, 0:HK]
        wg_sb = gate_in[:, 0:HK * E].rearrange("p (k e) -> p k e", k=HK)
        wgf = gate_in[:, HK * E:2 * HK * E].rearrange("p (k e) -> p k e", k=HK)
        condT_sb = gate_in[0:G, P:P + NB]
        gg_sb = y[0][0:G, 1 * E:2 * E]
        wgb_sb = y[0][0:NB, 2 * E:3 * E]
        ggb_sb = y[0][0:NB, 3 * E:4 * E]
        gb = y[0][0:NB, 4 * E:5 * E]
        gb_col = sb("gb_col", [NB, CW])
        sumsq = small[:, 12 * C:13 * C]
        mean_sq = small[:, 13 * C:14 * C]
        root = small[:, 14 * C:15 * C]
        rs = small[:, 15 * C:16 * C]
        tmp_c = small[:, 16 * C:17 * C]
        zero = sb("zero", [P, 1])
        prob = tmp(CW)
        rest = tmp(CW)
        t8 = tmp(CW)
        is_first = tmp(CW)
        is_second = tmp(CW)
        chosen16 = tmp(CW // 2).bitcast(BF16)
        top = small[:, 17 * C:18 * C]
        first = small[:, 18 * C:19 * C]
        second = small[:, 19 * C:20 * C]
        which = sb("which", [P, 2, C])
        pair_w = sb("pair_w", [P, 2, C])
        tot = tmp(CW)
        seg = tmp(CW)
        incl = tmp(CW)
        n_tiles = y[1][:, 0 * E:1 * E]
        tile_end = y[1][:, 1 * E:2 * E]
        one_e = y[1][:, 2 * E:3 * E]
        slot_at = tmp(CW)
        slot = small[:, 0 * C:2 * C].rearrange("p (k c) -> p k c", k=2)
        slot_t = small[:, 2 * C:4 * C].rearrange("p (k c) -> p k c", k=2)
        slot_r = small[:, 4 * C:6 * C].rearrange("p (k c) -> p k c", k=2)
        past = tmp(NT * (E - 1))
        tile_e = sb("tile_e", [P, NT], I32)
        tile_start = tmp(NT)
        pace = tmp(NT)
        pace_i = sb("pace_i", [P, NT + 1], I32)
        scatters_f = sb("scatters_f", [P, 2])
        twos_f = sb("twos_f", [P, 1])
        scatters_i = sb("scatters_i", [P, 2], I32)
        scatters = sb("scatters", [P, 2], I32)
        twos = sb("twos", [P, 1], I32)
        tab = tmp(2 * NT)
        tab_k = tmp(NT)
        tab_v = tmp(NT)
        tab_x = tmp(NT)
        take_row = sb("take_row", [P, NT + 3], I32)
        put_row = sb("put_row", [P, NT], I32)

        fw_sb = h1
        fw_pos = h2
        fw_q = sb("fw_q", [P, HK, H], BF16)
        fb_b = sb("fb_b", [P, H])
        fsum = sb("fsum", [P, 1])
        w_scale = sb("w_scale", [P, 1])
        thr = sb("thr", [P, 2])
        amax = sb("amax", [P, 4])
        amax1 = sb("amax1", [P, 1])
        amax_row = sb("amax_row", [1, 1])
        i_scale = sb("i_scale", [P, 1])
        i_inv = sb("i_inv", [P, 1])
        out_scale = sb("out_scale", [P, 1])
        magic = sb("magic", [P, 1])

        bank = [ctx.enter_context(nc.psum_tensor(f"bank{n}", [P, 512], F32)) for n in range(8)]
        p_l1, p_l2, p_l3, p_t0, p_t1, p_t2 = bank[:6]
        p_rank, p_total, p_table = bank[0], bank[1], bank[2]
        p_gate, p_small = bank[6], bank[7]
        p_qT = [bank[0], bank[1]]
        p_out = [[bank[2], bank[3]], [bank[4], bank[5]]]

        small_in = sem("small_in")
        ffn_in = sem("ffn_in")
        bias_in = sem("bias_in")
        feat_in = [sem(f"feat_in{n}") for n in range(4)]
        tok_in = [sem(f"tok_in{n}") for n in range(4)]
        expert_in = [sem(f"expert_in{n}") for n in range(2)]
        chunk_in = [sem(f"chunk_in{n}") for n in range(4)]
        weights_ready = sem("weights_ready")
        slots_ready = sem("slots_ready")
        in_tile_ready = sem("in_tile_ready")
        onehots_c = sem("onehots_c")
        rows_ready = sem("rows_ready")
        raw_ready = sem("raw_ready")
        chunks_rounded = sem("chunks_rounded")
        chunks_done = sem("chunks_done")
        pool_step = sem("pool_step")
        consts_ready = sem("consts_ready")
        vec_step = sem("vec_step")
        wgf_ready = sem("wgf_ready")
        cond_done = sem("cond_done")
        gb_ready = sem("gb_ready")
        gates_done = sem("gates_done")
        sumsq_done = sem("sumsq_done")
        mean_ready = sem("mean_ready")
        root_ready = sem("root_ready")
        logits_ready = sem("logits_ready")
        exp_done = sem("exp_done")
        chosen_ready = sem("chosen_ready")
        ranks_done = sem("ranks_done")
        onehots_p = sem("onehots_p")
        tables_done = sem("tables_done")
        routed = sem("routed")
        fsum_ready = sem("fsum_ready")
        fsum_done = sem("fsum_done")
        dma_go = sem("dma_go")
        take_set = sem("take_set")
        put_set = sem("put_set")
        gathered = [sem(f"gathered{n}") for n in range(2)]
        scattered = [sem(f"scattered{n}") for n in range(2)]
        t0_done, xt_ready = sem("t0_done"), sem("xt_ready")
        xt_rounded, h1T_rounded, h2T_rounded = sem("xt_rounded"), sem("h1T_rounded"), sem("h2T_rounded")
        l1_done, h1_ready, t1_done, h1T_ready = sem("l1_done"), sem("h1_ready"), sem("t1_done"), sem("h1T_ready")
        l2_done, h2_ready, t2_done, h2T_ready = sem("l2_done"), sem("h2_ready"), sem("t2_done"), sem("h2T_ready")
        l3_done, y_ready = sem("l3_done"), sem("y_ready")
        low_in = [sem(f"low_in{n}") for n in range(4)]
        high_in = [sem(f"high_in{n}") for n in range(4)]
        res_in = sem("res_in")
        low_scaled = sem("low_scaled")
        high_scaled = sem("high_scaled")
        high_summed = sem("high_summed")
        res_biased = sem("res_biased")
        amax_ready, amax_T, amax_one, amax_all, scales_ready = (
            sem("amax_ready"), sem("amax_T"), sem("amax_one"), sem("amax_all"), sem("scales_ready"))
        clipped = sem("clipped")
        rounded, q_ready, qT_done, qT_ready, ffn_done, res_ready = (
            sem("rounded"), sem("q_ready"), sem("qT_done"), sem("qT_ready"), sem("ffn_done"), sem("res_ready"))
        stored = [sem(f"stored{n}") for n in range(2)]

        PEEL = 4

        def turns(eng, body):
            for i in range(PEEL):
                body(0, i)
            with eng.Fori(0, FULL - PEEL // 2) as pair:
                body(pair, PEEL)
                body(pair, PEEL + 1)
            with eng.Fori(0, NT // 2 - FULL) as pair:
                used = eng.value_load(twos[0:1, 0:1], min_val=0, max_val=NT // 2 - FULL)
                with eng.If(pair < used):
                    body(pair, 2 * FULL)
                    body(pair, 2 * FULL + 1)
            used = eng.value_load(twos[0:1, 0:1], min_val=0, max_val=NT // 2 - FULL)
            body(used, 2 * FULL, True)
            body(used, 2 * FULL + 1, True)

        def is_tile(pair, n, last=False):
            return n < 2 * FULL if last else not isinstance(pair, int) or n >= 0

        def later(pair, n, first):
            return not isinstance(pair, int) or n >= first

        def groups(eng, body):
            body(0, 0)
            body(0, 1)
            with eng.Fori(0, NG // 2 - 3) as pair:
                body(pair, 2)
                body(pair, 3)
            for n in range(NG - 4, NG):
                body(0, n)

        def is_group(pair, n):
            return not isinstance(pair, int) or n < NG

        block = ctx.enter_context(nc.Block())
        QC = C // 4

        def quarter(ap, n):
            return ap[:, n * QC * H:(n + 1) * QC * H].rearrange("p (c h) -> p c h", c=QC)

        def token_rows(dram, first_row, n):
            return dram[first_row + n * QC * P:first_row + (n + 1) * QC * P, :].rearrange("(c p) h -> p c h", p=P)

        @block.sync
        def _(sp):
            for dst, src in ((rms_sb[:, :], rms), (wg_sb[:, :, :], wg.rearrange("(k p) e -> p k e", p=P)),
                             (condT_sb[:, :], condT), (gg_sb[:, :], gg), (wgb_sb[:, :], wgb.partition_broadcast(NB)),
                             (ggb_sb[:, :], ggb.partition_broadcast(NB))):
                sp.dma_start(dst, src).then_inc(small_in, 16)
            for n in range(4):
                sp.dma_start(x_feat[:, :, n * QC * P:(n + 1) * QC * P],
                             xT[:, n * QC * P:(n + 1) * QC * P].rearrange("(k p) t -> p k t", p=P)
                             ).then_inc(feat_in[n], 16)
                sp.dma_start(quarter(x_tok, n), token_rows(x, 0, n)).then_inc(tok_in[n], 16)
            def load_expert(e):
                sp.dma_start(stage[:, e * WE:(e + 1) * WE], w[:, e * WE:(e + 1) * WE]).then_inc(expert_in[e], 16)
                sp.wait_ge(expert_in[e], 16)
                sp.sem_inc(raw_ready, EC)

            def load_chunk(chunk, n):
                sp.wait_ge(chunks_done, chunk - (2 * EC - 1))
                sp.dma_start(stage[:, bass.ds(chunk % (2 * EC) * CH, CH)], w[:, bass.ds(chunk * CH, CH)]
                             ).then_inc(chunk_in[n], 16)

            load_expert(0)
            sp.wait_ge(weights_ready, 1)
            sp.wait_ge(gathered[1], 16)
            load_expert(1)
            for n in range(4):
                load_chunk(2 * EC + n, n)
            with sp.Fori(1, (E - 2) * EC // 4) as four:
                for n in range(4):
                    sp.wait_ge(chunk_in[n], four * 16)
                    sp.sem_inc(raw_ready, 1)
                    load_chunk(four * 4 + (2 * EC + n), n)
            for n in range(4):
                sp.wait_ge(chunk_in[n], (E - 2) * EC // 4 * 16)
                sp.sem_inc(raw_ready, 1)
            low_rows = sp.value_load(scatters[0:1, 0:1], min_val=16, max_val=8 * NT)
            sp.wait_ge(scattered[0], low_rows)
            sp.wait_ge(scattered[1], low_rows)
            for n in range(4):
                sp.dma_start(quarter(y_low, n), token_rows(pair_rows, 0, n)).then_inc(low_in[n], 16)
                sp.wait_ge(low_in[n], 16)
            for n in range(4):
                sp.dma_start(quarter(x_res, n), token_rows(x, 0, n)).then_inc(res_in, 16)
                sp.wait_ge(res_in, 16 * (n + 1))
            all_rows = sp.value_load(scatters[0:1, 1:2], min_val=16 * FULL, max_val=8 * NT)
            sp.wait_ge(scattered[0], all_rows)
            sp.wait_ge(scattered[1], all_rows)
            for n in range(4):
                sp.dma_start(quarter(y_high, n), token_rows(pair_rows, T, n)).then_inc(high_in[n], 16)
            out_v = out.rearrange("(g c p) h -> p g c h", p=P, c=CG)
            with sp.Fori(0, NG // 2) as turn:
                for n in range(2):
                    sp.wait_ge(res_ready, 2 * turn + n + 1)
                    sp.dma_start(out_v[:, bass.ds(2 * turn + n, 1), :, :].rearrange("p g c h -> p (g c) h"),
                                 res[n][:, :].rearrange("p (c h) -> p c h", c=CG)).then_inc(stored[n], 16)
            for n in range(2):
                sp.wait_ge(stored[n], 16 * (NG // 2))

        @block.gpsimd
        def _(pool):
            steps = [0]

            def step(ins):
                steps[0] += 1
                ins.then_inc(pool_step, 1)
                pool.wait_ge(pool_step, steps[0])

            for dst, value in ((ident, 0.0), (ident16, 0.0), (earlier, 1.0), (batch_half, 0.0), (batch_col, 0.0),
                               (ones16, 1.0), (ones32, 1.0)):
                step(nc.gpsimd.memset(dst[:, :], value))
            for m in (ident, ident16):
                step(nc.gpsimd.affine_select(out=m[:, :], in_=m[:, :], compare_op=ALU.not_equal, fill=1.0, base=0,
                                             pattern=[[-1, P]], channel_multiplier=1))
            step(nc.gpsimd.affine_select(out=earlier[:, :], in_=earlier[:, :], compare_op=ALU.is_gt, fill=0.0, base=0,
                                         pattern=[[1, P]], channel_multiplier=-1))
            step(nc.gpsimd.memset(batch_half[0:C, 0:SB], 1.0))
            step(nc.gpsimd.memset(batch_half[C:2 * C, SB:P], 1.0))
            for h in range(2):
                step(nc.gpsimd.affine_select(out=batch_col[:, :], in_=batch_col[:, :], compare_op=ALU.not_equal,
                                             fill=1.0, base=-h * C, pattern=[[-1, C]], channel_multiplier=1))

            def count(out_ap, pattern, base=0, mult=0):
                return nc.gpsimd.iota(out_ap, pattern=pattern, base=base, channel_multiplier=mult,
                                      allow_small_or_imprecise_dtypes=True)

            step(count(count_r[:, :], [[1, P]]))
            step(count(count_t[:, :], [[1, NT]]))
            step(count(count_e[:, :], [[1, E]], base=-E))
            step(count(col_no[:, :], [[1, 2 * C]], base=1))
            step(count(part_no[:, :], [[0, 1]], mult=1))
            step(count(dummy_no[:, :].rearrange("p (a b) -> p a b", b=2), [[0, NT // 2], [P, 2]],
                       base=DUMMY + P, mult=1))
            pool.sem_inc(consts_ready, 1)

            def split(chunk):
                at = chunk % (RING * EC) * (2 * CH)
                nc.gpsimd.tensor_tensor(ring[:, bass.ds(at + CH, CH)], stage[:, bass.ds(chunk % (2 * EC) * CH, CH)],
                                        ring[:, bass.ds(at, CH)].bitcast(F32), ALU.subtract).then_inc(chunks_done, 1)

            pool.wait_ge(chunks_rounded, EC)
            for chunk in range(EC):
                split(chunk)

            for k in range(2):
                pool.wait_ge(in_tile_ready, k + 1)
                nc.gpsimd.tensor_tensor(onehot_t[k][:, :, 0, :], is_in_tile[k],
                                        col_no[:, k * C:(k + 1) * C].unsqueeze(2).to_broadcast([P, C, NT]), ALU.mult
                                        ).then_inc(onehots_c, 1)

            pool.wait_ge(routed, 1)

            def gather(pair, n):
                i, b = 2 * pair + n, n % 2
                if later(pair, n, 2):
                    pool.wait_ge(t0_done, i - 1)
                nc.gpsimd.tensor_copy(take_now[b][:, :], take_row[:, bass.ds(i, 1)]).then_inc(take_set, 1)
                pool.wait_ge(take_set, i + 1)
                pool.sem_inc(dma_go, 1)
                nc.gpsimd.indirect_dma_start(
                    rows[b][:, :], None, x, bass.IndirectOffsetOnAxis(ap=take_now[b][:, 0:1].bitcast(U32), axis=0)
                ).then_inc(gathered[b], 16)

            def scatter(pair, n):
                i, b = 2 * pair + n, n % 2
                if later(pair, n, 2):
                    pool.wait_ge(scattered[b], 16 * (pair + n // 2))
                nc.gpsimd.tensor_copy(put_now[b][:, :], put_row[:, bass.ds(i, 1)]).then_inc(put_set, 1)
                pool.wait_ge(put_set, i + 1)
                pool.wait_ge(y_ready, i + 1)
                pool.sem_inc(dma_go, 1)
                nc.gpsimd.indirect_dma_start(
                    pair_rows, bass.IndirectOffsetOnAxis(ap=put_now[b][:, 0:1].bitcast(U32), axis=0), y[b][:, :], None
                ).then_inc(scattered[b], 16)

            for i in range(3):
                gather(0, i)

            def split_some(pair, n):
                i = 2 * pair + n
                done = pool.value_load(pace_i[0:1, bass.ds(i, 1)], min_val=0, max_val=EC * E)
                goal = pool.value_load(pace_i[0:1, bass.ds(i + 1, 1)], min_val=0, max_val=EC * E)
                with pool.If(done < goal):
                    with pool.Fori(done, goal) as chunk:
                        pool.wait_ge(chunks_rounded, chunk + 1)
                        split(chunk)

            def turn(pair, n, last=False):
                if is_tile(pair, n + 3, last):
                    gather(pair, n + 3)
                if is_tile(pair, n - 2, last):
                    scatter(pair, n - 2)
                if is_tile(pair, n, last):
                    split_some(pair, n)

            turns(pool, turn)

            pool.wait_ge(res_in, 64)
            pool.wait_ge(ffn_in, 32)
            xr = x_res.rearrange("p (c h) -> p c h", c=C)

            def bias_quarter(n):
                part = xr[:, n * QC:(n + 1) * QC, :]
                nc.gpsimd.tensor_tensor(part, part, fb_b[:, :].unsqueeze(1).to_broadcast([P, QC, H]),
                                        ALU.add).then_inc(res_biased, 1)

            bias_quarter(0)
            bias_quarter(1)
            pool.wait_ge(low_scaled, 4)
            pool.wait_ge(high_scaled, 1)
            last = slice(3 * QC * H, C * H)
            nc.gpsimd.tensor_tensor(y_high[:, last], y_high[:, last], y_low[:, last], ALU.add).then_inc(high_summed, 1)
            bias_quarter(2)
            bias_quarter(3)

        @block.scalar
        def _(act):
            act.dma_start(fw_sb[:, :].rearrange("p (k o) -> p k o", k=HK),
                          fwT.rearrange("(k p) o -> p k o", p=P)).then_inc(ffn_in, 16)
            act.dma_start(fb_b[:, :], fbias.partition_broadcast(P)).then_inc(ffn_in, 16)
            for n in range(4):
                act.wait_ge(tok_in[n], 16)
                for c in range(n * QC, (n + 1) * QC):
                    part = x_tok[:, c * H:(c + 1) * H]
                    last = nc.scalar.activation(part, part, ACT.Square, accum_out=sumsq[:, c:c + 1])
            last.then_inc(sumsq_done, 1)
            for dst, src in ((b1_b, b1), (b2_b, b2), (b3_b, b3)):
                act.dma_start(dst[:, :], src.rearrange("e m -> (e m)").partition_broadcast(P)).then_inc(bias_in, 16)
            act.wait_ge(mean_ready, 1)
            nc.scalar.activation(root[:, :], mean_sq[:, :], ACT.Sqrt).then_inc(root_ready, 1)
            def round_chunk(chunk):
                nc.scalar.activation(ring[:, bass.ds(chunk % (RING * EC) * (2 * CH), CH)],
                                     stage[:, bass.ds(chunk % (2 * EC) * CH, CH)], ACT.Copy).then_inc(chunks_rounded, 1)

            act.wait_ge(raw_ready, EC)
            for chunk in range(EC):
                round_chunk(chunk)
            for k in range(2):
                act.wait_ge(in_tile_ready, k + 1)
                nc.scalar.activation(onehot_t[k][:, :, 1, :], is_in_tile[k], ACT.Copy,
                                     scale=part_no[:, 0:1]).then_inc(onehots_p, 1)
            act.wait_ge(logits_ready, 1)
            nc.scalar.activation(prob[:, :], prob[:, :], ACT.Exp).then_inc(exp_done, 1)

            def turn(pair, n, last=False):
                i, b = 2 * pair + n, n % 2
                if is_tile(pair, n - 2, last):
                    act.wait_ge(t2_done, i - 1)
                    if later(pair, n, 4):
                        act.wait_ge(l3_done, i - 3)
                    nc.scalar.activation(h2T[b][0][:, :], p_t2[:, :], ACT.Relu).then_inc(h2T_rounded, 1)
                if is_tile(pair, n + 1, last):
                    act.wait_ge(t0_done, i + 2)
                    nc.scalar.activation(xt[0][:, :], p_t0[:, 0:H], ACT.Copy).then_inc(xt_rounded, 1)
                if is_tile(pair, n, last):
                    act.wait_ge(t1_done, i + 1)
                    if later(pair, n, 2):
                        act.wait_ge(l2_done, i - 1)
                    nc.scalar.activation(h1T[b][0][:, :], p_t1[:, :], ACT.Relu).then_inc(h1T_rounded, 1)
                    done = act.value_load(pace_i[0:1, bass.ds(i, 1)], min_val=0, max_val=EC * E)
                    goal = act.value_load(pace_i[0:1, bass.ds(i + 1, 1)], min_val=0, max_val=EC * E)
                    with act.If(done < goal):
                        if later(pair, n, 2):
                            act.wait_ge(l3_done, i - 1)
                        with act.Fori(done, goal) as chunk:
                            act.wait_ge(raw_ready, chunk + 1)
                            round_chunk(chunk)

            act.wait_ge(t0_done, 1)
            nc.scalar.activation(xt[0][:, :], p_t0[:, 0:H], ACT.Copy).then_inc(xt_rounded, 1)
            turns(act, turn)

            for n in range(4):
                act.wait_ge(low_in[n], 16)
                for c in range(n * QC, (n + 1) * QC):
                    part = y_low[:, c * H:(c + 1) * H]
                    last = nc.scalar.activation(part, part, ACT.Copy, scale=pair_w[:, 0, c:c + 1])
                last.then_inc(low_scaled, 1)
            act.wait_ge(high_in[3], 16)
            for c in range(3 * QC, C):
                part = y_high[:, c * H:(c + 1) * H]
                last = nc.scalar.activation(part, part, ACT.Copy, scale=pair_w[:, 1, c:c + 1])
            last.then_inc(high_scaled, 1)

            def integers(pair, n):
                g, b = 2 * pair + n, n % 2
                act.wait_ge(clipped, g + 1)
                if later(pair, n, 2):
                    act.wait_ge(qT_done, g - 1)
                nc.scalar.activation(q16[b][:, :], y_high[:, bass.ds(g * CG * H, CG * H)], ACT.Identity,
                                     bias=magic[:, 0:1]).then_inc(q_ready, 1)

            def group(pair, n):
                g, b = 2 * pair + n, n % 2
                if is_group(pair, n + 1):
                    integers(pair, n + 1)
                act.wait_ge(qT_done, g + 1)
                if later(pair, n, 2):
                    act.wait_ge(ffn_done, g - 1)
                nc.scalar.activation(qT[b][:, :], p_qT[b][:, :].bitcast(BF16), ACT.Copy).then_inc(qT_ready, 1)

            integers(0, 0)
            groups(act, group)

        @block.vector
        def _(dve):
            steps = [0]
            V = nc.vector

            def step(ins):
                steps[0] += 1
                ins.then_inc(vec_step, 1)
                dve.wait_ge(vec_step, steps[0])

            def by_ce(ap):
                return ap.rearrange("p (c e) -> p c e", e=E)

            def over_e(ap):
                return ap.unsqueeze(2).to_broadcast([P, C, E])

            e_of = count_e[:, :].unsqueeze(1).to_broadcast([P, C, E])

            step(V.memset(magic[:, :], -MAGIC))
            step(V.memset(one_e[:, :], 1.0))
            step(V.memset(seg[:, :], 1.0))
            step(V.memset(seg[:, :].rearrange("p (e c) -> p e c", e=E)[:, :, 0:1], 0.0))
            dve.wait_ge(small_in, 16 * 6)
            for k in range(HK):
                step(V.tensor_scalar(wgf[:, k, :], wg_sb[:, k, :], rms_sb[:, k:k + 1], None, ALU.mult))
            V.memset(zero[:, :], 0.0).then_inc(wgf_ready, 1)
            dve.wait_ge(cond_done, 1)
            dve.wait_ge(consts_ready, 1)
            step(V.tensor_tensor(gb[:, :], p_small[0:NB, 0:E], wgb_sb[:, :], ALU.add))
            step(V.tensor_tensor(gb[:, :], gb[:, :], ggb_sb[:, :], ALU.add))
            V.tensor_tensor(gb_col[:, :].rearrange("p (c e) -> p c e", e=E),
                            gb[:, :].unsqueeze(1).to_broadcast([NB, C, E]),
                            batch_col[:, :].unsqueeze(2).to_broadcast([NB, C, E]), ALU.mult).then_inc(gb_ready, 1)
            dve.wait_ge(ffn_in, 32)
            V.tensor_reduce(fsum[:, :], fw_sb[:, :], AX.X, ALU.add, apply_absolute_value=True).then_inc(fsum_ready, 1)
            dve.wait_ge(fsum_done, 1)
            step(V.tensor_scalar(w_scale[:, :], p_small[:, 16:17], 1.0 / (H * H), None, ALU.mult))
            step(V.tensor_scalar(thr[:, 0:1], w_scale[:, :], 0.5, None, ALU.mult))
            step(V.tensor_scalar(thr[:, 1:2], w_scale[:, :], -0.5, None, ALU.mult))
            step(V.tensor_scalar(fw_pos[:, :], fw_sb[:, :], thr[:, 0:1], None, ALU.is_gt))
            step(V.scalar_tensor_tensor(fw_pos[:, :], fw_sb[:, :], thr[:, 1:2], fw_pos[:, :], ALU.is_lt, ALU.subtract))
            step(V.tensor_scalar(fw_q[:, :, :].rearrange("p k o -> p (k o)"), fw_pos[:, :], -1.0, None, ALU.mult))

            dve.wait_ge(sumsq_done, 1)
            V.tensor_scalar(mean_sq[:, :], sumsq[:, :], 1.0 / H, 1e-6, ALU.mult, ALU.add).then_inc(mean_ready, 1)
            dve.wait_ge(root_ready, 1)
            step(V.reciprocal(rs[:, :], root[:, :]))
            step(V.tensor_tensor(tmp_c[:, :], rs[:, :], rs[:, :], ALU.mult))
            step(V.tensor_tensor(tmp_c[:, :], tmp_c[:, :], mean_sq[:, :], ALU.mult))
            step(V.tensor_scalar(tmp_c[:, :], tmp_c[:, :], -0.5, 1.5, ALU.mult, ALU.add))
            step(V.tensor_tensor(rs[:, :], rs[:, :], tmp_c[:, :], ALU.mult))

            dve.wait_ge(gates_done, 1)
            step(V.tensor_tensor(by_ce(prob[:, :]), by_ce(p_gate[:, 0:CW]), over_e(rs[:, :]), ALU.mult))
            step(V.tensor_tensor(prob[:, :], prob[:, :], p_gate[:, CW:2 * CW], ALU.add))

            def largest(values, peak, number, onehot):
                step(V.tensor_reduce(peak[:, :], by_ce(values[:, :]), AX.X, ALU.max))
                step(V.tensor_tensor(by_ce(t8[:, :]), by_ce(values[:, :]), over_e(peak[:, :]), ALU.is_equal))
                step(V.tensor_tensor(by_ce(t8[:, :]), by_ce(t8[:, :]), e_of, ALU.mult))
                step(V.tensor_reduce(number[:, :], by_ce(t8[:, :]), AX.X, ALU.min))
                step(V.tensor_tensor(by_ce(onehot[:, :]), e_of, over_e(number[:, :]), ALU.is_equal))

            largest(prob, top, first, is_first)
            step(V.scalar_tensor_tensor(rest[:, :], is_first[:, :], -3e38, prob[:, :], ALU.mult, ALU.add))
            largest(rest, tmp_c, second, is_second)
            V.tensor_tensor(chosen16[:, :], is_first[:, :], is_second[:, :], ALU.add).then_inc(chosen_ready, 1)
            step(V.tensor_tensor(which[:, 0, :], first[:, :], second[:, :], ALU.min))
            step(V.tensor_tensor(which[:, 1, :], first[:, :], second[:, :], ALU.max))
            step(V.tensor_tensor(by_ce(is_first[:, :]), e_of, over_e(which[:, 0, :]), ALU.is_equal))
            step(V.tensor_tensor(by_ce(is_second[:, :]), e_of, over_e(which[:, 1, :]), ALU.is_equal))

            def pick(dst, onehot, values):
                step(V.tensor_tensor(t8[:, :], onehot[:, :], values[:, :], ALU.mult))
                step(V.tensor_reduce(dst, by_ce(t8[:, :]), AX.X, ALU.add))

            dve.wait_ge(ranks_done, 1)
            step(V.tensor_copy(tot[:, :].rearrange("p (e c) -> p e c", e=E),
                               p_total[:, 0:CW].rearrange("p (c e) -> p e c", e=E)))
            step(V.tensor_tensor_scan(incl[:, :], seg[:, :], tot[:, :], 0.0, ALU.mult, ALU.add))
            in_expert = incl[:, :].rearrange("p (e c) -> p e c", e=E)
            step(V.tensor_scalar(n_tiles[:, :].unsqueeze(2), in_expert[:, :, C - 1:C], 1.0 / P, 0.5 - 0.5 / P, ALU.mult, ALU.add))
            step(V.tensor_scalar(n_tiles[:, :], n_tiles[:, :], MAGIC, MAGIC, ALU.add, ALU.subtract))
            step(V.tensor_scalar(n_tiles[:, :], n_tiles[:, :], 1.0, None, ALU.max))
            step(V.tensor_tensor_scan(tile_end[:, :], one_e[:, :], n_tiles[:, :], 0.0, ALU.mult, ALU.add))
            step(V.tensor_tensor(n_tiles[:, :], tile_end[:, :], n_tiles[:, :], ALU.subtract))
            step(V.tensor_tensor(tot[:, :], incl[:, :], tot[:, :], ALU.subtract))
            step(V.tensor_tensor(by_ce(slot_at[:, :]), by_ce(p_rank[:, 0:CW]),
                                 tot[:, :].rearrange("p (e c) -> p c e", e=E), ALU.add))
            step(V.scalar_tensor_tensor(by_ce(slot_at[:, :]), n_tiles[:, :].unsqueeze(1).to_broadcast([P, C, E]),
                                        float(P), by_ce(slot_at[:, :]), ALU.mult, ALU.add))
            pick(slot[:, 0, :], is_first, slot_at)
            pick(slot[:, 1, :], is_second, slot_at)
            step(V.tensor_scalar(slot_t[:, :, :], slot[:, :, :], 1.0 / P, 0.5 / P - 0.5, ALU.mult, ALU.add))
            step(V.tensor_scalar(slot_t[:, :, :], slot_t[:, :, :], MAGIC, MAGIC, ALU.add, ALU.subtract))
            V.scalar_tensor_tensor(slot_r[:, :, :], slot_t[:, :, :], -float(P), slot[:, :, :], ALU.mult, ALU.add
                                   ).then_inc(slots_ready, 1)
            dve.wait_ge(slots_ready, 1)

            for k in range(2):
                V.tensor_tensor(is_in_tile[k], slot_t[:, k, :].unsqueeze(2).to_broadcast([P, C, NT]),
                                count_t[:, :].unsqueeze(1).to_broadcast([P, C, NT]), ALU.is_equal
                                ).then_inc(in_tile_ready, 1)
            for k in range(2):
                for c in range(0, C, C // 2):
                    V.tensor_tensor(onehot_r[k][:, c:c + C // 2, :],
                                    slot_r[:, k, c:c + C // 2].unsqueeze(2).to_broadcast([P, C // 2, P]),
                                    count_r[:, :].unsqueeze(1).to_broadcast([P, C // 2, P]), ALU.is_equal
                                    ).then_inc(rows_ready, 1)

            step(V.tensor_tensor(past[:, :].rearrange("p (t e) -> p t e", t=NT),
                                 count_t[:, :].unsqueeze(2).to_broadcast([P, NT, E - 1]),
                                 tile_end[:, 0:E - 1].unsqueeze(1).to_broadcast([P, NT, E - 1]), ALU.is_ge))
            step(V.tensor_reduce(tab_x[:, :], past[:, :].rearrange("p (t e) -> p t e", t=NT), AX.X, ALU.add))
            step(V.tensor_copy(tile_e[:, :], tab_x[:, :]))
            step(V.tensor_tensor(past[:, :].rearrange("p (t e) -> p t e", t=NT), past[:, :].rearrange("p (t e) -> p t e", t=NT),
                                 tile_end[:, 0:E - 1].unsqueeze(1).to_broadcast([P, NT, E - 1]), ALU.mult))
            step(V.tensor_reduce(tile_start[:, :], past[:, :].rearrange("p (t e) -> p t e", t=NT), AX.X, ALU.max))
            step(V.tensor_tensor(pace[:, :], count_t[:, :], tile_start[:, :], ALU.subtract))
            step(V.tensor_scalar(pace[:, :], pace[:, :], 2.0, float(EC), ALU.mult, ALU.min))
            step(V.tensor_scalar(tab_x[:, :], tab_x[:, :], float(EC), float(EC), ALU.mult, ALU.add))
            step(V.tensor_tensor(pace[:, :], pace[:, :], tab_x[:, :], ALU.add))
            step(V.tensor_tensor(pace[:, 0:NT - 1], pace[:, 0:NT - 1], tab_x[:, 1:NT], ALU.max))
            step(V.memset(pace_i[:, 0:1], EC))
            step(V.tensor_scalar(pace_i[:, 1:NT + 1], pace[:, :], float(EC * E), None, ALU.min))
            step(V.tensor_scalar(scatters_f[:, :], tile_end[:, E - 2:E], 8.0, 8.0, ALU.mult, ALU.add))
            step(V.tensor_copy(scatters_i[:, :], scatters_f[:, :]))
            step(V.tensor_scalar(scatters[:, :], scatters_i[:, :], -16, None, ALU.bitwise_and))
            step(V.tensor_scalar(twos_f[:, :], scatters[:, 1:2], 1.0 / 16, -float(FULL), ALU.mult, ALU.add))
            step(V.tensor_copy(twos[:, :], twos_f[:, :]))
            step(V.memset(take_row[:, NT:NT + 3], 0))

            dve.wait_ge(tables_done, 1)
            step(V.tensor_copy(tab[:, :], p_table[:, 0:2 * NT]))
            a, b_ = tab[:, 0:NT], tab[:, NT:2 * NT]
            step(V.scalar_tensor_tensor(tab_x[:, :], a, float(P), b_, ALU.mult, ALU.add))
            step(V.tensor_scalar(tab_k[:, :], a, C + 0.5, None, ALU.is_gt))
            step(V.scalar_tensor_tensor(tab_k[:, :], tab_k[:, :], -float(T), tab_x[:, :], ALU.mult, ALU.add))
            step(V.tensor_scalar(take_row[:, 0:NT], tab_k[:, :], -float(P), 0.0, ALU.add, ALU.max))
            step(V.tensor_scalar(tab_v[:, :], a, 0.5, None, ALU.is_lt))
            step(V.tensor_tensor(tab_v[:, :], tab_v[:, :], dummy_no[:, :], ALU.mult))
            step(V.tensor_tensor(tab_x[:, :], tab_x[:, :], tab_v[:, :], ALU.add))
            V.tensor_scalar(put_row[:, :], tab_x[:, :], -float(P), None, ALU.add).then_inc(routed, 1)

            V.tensor_tensor(by_ce(prob[:, :]), by_ce(prob[:, :]), over_e(top[:, :]), ALU.subtract).then_inc(logits_ready, 1)
            dve.wait_ge(exp_done, 1)
            step(V.tensor_reduce(top[:, :], by_ce(prob[:, :]), AX.X, ALU.add))
            step(V.reciprocal(top[:, :], top[:, :]))
            step(V.tensor_tensor(by_ce(prob[:, :]), by_ce(prob[:, :]), over_e(top[:, :]), ALU.mult))
            pick(pair_w[:, 0, :], is_first, prob)
            pick(pair_w[:, 1, :], is_second, prob)
            dve.sem_inc(weights_ready, 1)

            dve.wait_ge(routed, 1)
            dve.wait_ge(bias_in, 48)

            def expert(pair, n):
                return dve.value_load(tile_e[0:1, bass.ds(2 * pair + n, 1)], min_val=0, max_val=E - 1)

            def rest_of(dst, psum, ready, relu):
                if relu:
                    V.scalar_tensor_tensor(dst[1][:, :], psum, 0.0, dst[0][:, :].bitcast(F32),
                                           ALU.max, ALU.subtract).then_inc(ready, 1)
                else:
                    V.tensor_tensor(dst[1][:, :], psum, dst[0][:, :].bitcast(F32), ALU.subtract).then_inc(ready, 1)

            def turn(pair, n, last=False):
                i, b = 2 * pair + n, n % 2
                if is_tile(pair, n, last):
                    e = expert(pair, n)
                    dve.wait_ge(l1_done, i + 1)
                    if later(pair, n, 1):
                        dve.wait_ge(t1_done, i)
                    V.tensor_tensor(h1[:, :], p_l1[:, :], b1_b[:, bass.ds(e * M, M)],
                                    ALU.add).then_inc(h1_ready, 1)
                if is_tile(pair, n - 2, last):
                    dve.wait_ge(h2T_rounded, i - 1)
                    rest_of(h2T[b], p_t2[:, :], h2T_ready, True)
                if is_tile(pair, n + 1, last):
                    dve.wait_ge(xt_rounded, i + 2)
                    rest_of(xt, p_t0[:, 0:H], xt_ready, False)
                if is_tile(pair, n - 1, last):
                    e = expert(pair, n - 1)
                    dve.wait_ge(l2_done, i)
                    if later(pair, n, 2):
                        dve.wait_ge(t2_done, i - 1)
                    V.tensor_tensor(h2[:, :], p_l2[:, :], b2_b[:, bass.ds(e * M, M)],
                                    ALU.add).then_inc(h2_ready, 1)
                if is_tile(pair, n, last):
                    dve.wait_ge(h1T_rounded, i + 1)
                    rest_of(h1T[b], p_t1[:, :], h1T_ready, True)
                if is_tile(pair, n - 2, last):
                    e = expert(pair, n - 2)
                    dve.wait_ge(l3_done, i - 1)
                    if later(pair, n, 4):
                        dve.wait_ge(scattered[b], 16 * (pair + (n - 2) // 2))
                    V.tensor_tensor(y[b][:, :], p_l3[:, 0:H], b3_b[:, bass.ds(e * H, H)],
                                    ALU.add).then_inc(y_ready, 1)

            dve.wait_ge(xt_rounded, 1)
            rest_of(xt, p_t0[:, 0:H], xt_ready, False)
            turns(dve, turn)

            for n in range(4):
                part = slice(n * QC * H, (n + 1) * QC * H)
                if n < 3:
                    dve.wait_ge(high_in[n], 16)
                    dve.wait_ge(low_scaled, n + 1)
                    for c in range(n * QC, (n + 1) * QC):
                        col = slice(c * H, (c + 1) * H)
                        last = V.scalar_tensor_tensor(y_high[:, col], y_high[:, col], pair_w[:, 1, c:c + 1],
                                                      y_low[:, col], ALU.mult, ALU.add)
                    step(last)
                else:
                    dve.wait_ge(high_summed, 1)
                step(V.tensor_reduce(amax[:, n:n + 1], y_high[:, part], AX.X, ALU.max, apply_absolute_value=True))
            V.tensor_reduce(amax1[:, :], amax[:, :], AX.X, ALU.max).then_inc(amax_ready, 1)
            dve.wait_ge(amax_T, 1)
            V.tensor_reduce(amax_row[:, :], p_small[0:1, 0:P], AX.X, ALU.max).then_inc(amax_one, 1)
            dve.wait_ge(amax_all, 1)
            step(V.tensor_scalar(i_scale[:, :], p_small[:, 0:1], 1.0 / 127.0, None, ALU.mult))
            step(V.reciprocal(i_inv[:, :], i_scale[:, :]))
            step(V.tensor_tensor(out_scale[:, :], w_scale[:, :], i_scale[:, :], ALU.mult))

            def scale(pair, n):
                part = y_high[:, bass.ds((2 * pair + n) * CG * H, CG * H)]
                V.tensor_scalar(part, part, i_inv[:, 0:1], MAGIC, ALU.mult, ALU.add).then_inc(rounded, 1)

            def clip(pair, n):
                part = y_high[:, bass.ds((2 * pair + n) * CG * H, CG * H)]
                dve.wait_ge(rounded, 2 * pair + n + 1)
                V.tensor_scalar(part, part, MAGIC - 128.0, MAGIC + 127.0, ALU.max, ALU.min).then_inc(clipped, 1)

            def group(pair, n):
                g, b = 2 * pair + n, n % 2
                if is_group(pair, n + 3):
                    scale(pair, n + 3)
                dve.wait_ge(ffn_done, g + 1)
                dve.wait_ge(res_biased, pair + n // 2 + 1)
                if later(pair, n, 2):
                    dve.wait_ge(stored[b], 16 * (pair + n // 2))
                for h in range(2):
                    last = V.scalar_tensor_tensor(
                        res[b][:, h * 2 * H:(h + 1) * 2 * H], p_out[b][h][:, :], out_scale[:, 0:1],
                        x_res[:, bass.ds(g * CG * H + h * 2 * H, 2 * H)], ALU.mult, ALU.add)
                last.then_inc(res_ready, 1)
                if is_group(pair, n + 3):
                    clip(pair, n + 3)

            scale(0, 0)
            for n in range(3):
                if n < 2:
                    scale(0, n + 1)
                clip(0, n)
            groups(dve, group)

        @block.tensor
        def _(pe):
            PE = nc.tensor
            pe.wait_ge(small_in, 16 * 6)
            pe.wait_ge(consts_ready, 1)
            PE.matmul(p_small[0:NB, 0:E], condT_sb[:, :], gg_sb[:, :], start=True, stop=True).then_inc(cond_done, 1)
            pe.wait_ge(fsum_ready, 1)
            PE.matmul(p_small[:, 16:17], ones32[:, :], fsum[:, :], start=True, stop=True).then_inc(fsum_done, 1)
            pe.wait_ge(wgf_ready, 1)
            for n in range(4):
                pe.wait_ge(feat_in[n], 16)
                for c in range(n * QC, (n + 1) * QC):
                    for k in range(HK):
                        PE.matmul(p_gate[:, c * E:(c + 1) * E], x_feat[:, k, c * P:(c + 1) * P], wgf[:, k, :],
                                  start=(k == 0), stop=(k == HK - 1))
            pe.wait_ge(gb_ready, 1)
            PE.matmul(p_gate[:, CW:2 * CW], batch_half[:, :], gb_col[:, :], start=True, stop=True).then_inc(gates_done, 1)
            pe.wait_ge(chosen_ready, 1)
            PE.matmul(p_rank[:, 0:CW], earlier[:, :], chosen16[:, :], start=True, stop=True)
            PE.matmul(p_total[:, 0:CW], ones16[:, :], chosen16[:, :], start=True, stop=True).then_inc(ranks_done, 1)
            for k in range(2):
                pe.wait_ge(onehots_c, k + 1)
                pe.wait_ge(onehots_p, k + 1)
                for c in range(C):
                    if c % (C // 2) == 0:
                        pe.wait_ge(rows_ready, 2 * k + 2 * c // C + 1)
                    last = PE.matmul(p_table[:, 0:2 * NT], onehot_r[k][:, c, :],
                                     onehot_t[k][:, c, :, :].rearrange("p v t -> p (v t)"),
                                     start=(k == 0 and c == 0), stop=(k == 1 and c == C - 1))
            last.then_inc(tables_done, 1)

            pe.wait_ge(routed, 1)

            def expert(pair, n):
                return pe.value_load(tile_e[0:1, bass.ds(2 * pair + n, 1)], min_val=0, max_val=E - 1)

            def product(psum, lhs, chunks, width, e, first, done):
                slot_at = e % RING * SLOT
                for k in range(chunks):
                    at = 2 * CH * (first + k * width // CH) + k * width % CH
                    rounded = ring[:, bass.ds(slot_at + at, width)]
                    rest = ring[:, bass.ds(slot_at + (at + CH), width)]
                    part = [t[:, k * P:(k + 1) * P] for t in lhs]
                    PE.matmul(psum[:, 0:width], part[1], rounded, start=(k == 0), stop=False)
                    PE.matmul(psum[:, 0:width], part[0], rest, start=False, stop=False)
                    last = PE.matmul(psum[:, 0:width], part[0], rounded, start=False, stop=(k == chunks - 1))
                last.then_inc(done, 1)

            def transposes(psum, src, chunks, done):
                for k in range(chunks):
                    last = PE.transpose(psum[:, k * P:(k + 1) * P], src[:, k * P:(k + 1) * P], ident[:, :])
                last.then_inc(done, 1)

            def transpose_rows(pair, n):
                pe.wait_ge(gathered[n % 2], 16 * (pair + n // 2 + 1))
                if later(pair, n, 1):
                    pe.wait_ge(xt_ready, 2 * pair + n)
                transposes(p_t0, rows[n % 2], HK, t0_done)

            def turn(pair, n, last=False):
                i, b = 2 * pair + n, n % 2
                if is_tile(pair, n, last):
                    e = expert(pair, n)
                    pe.wait_ge(chunks_done, (e + 1) * EC)
                    pe.wait_ge(xt_ready, i + 1)
                    if later(pair, n, 1):
                        pe.wait_ge(h1_ready, i)
                    product(p_l1, xt, HK, M, e, 0, l1_done)
                if is_tile(pair, n - 2, last):
                    pe.wait_ge(h2_ready, i - 1)
                    if later(pair, n, 3):
                        pe.wait_ge(h2T_ready, i - 2)
                    transposes(p_t2, h2, MK, t2_done)
                if is_tile(pair, n + 1, last):
                    transpose_rows(pair, n + 1)
                if is_tile(pair, n - 1, last):
                    e2 = expert(pair, n - 1)
                    pe.wait_ge(h1T_ready, i)
                    if later(pair, n, 2):
                        pe.wait_ge(h2_ready, i - 1)
                    product(p_l2, h1T[1 - b], MK, M, e2, W2O // CH, l2_done)
                if is_tile(pair, n, last):
                    pe.wait_ge(h1_ready, i + 1)
                    if later(pair, n, 1):
                        pe.wait_ge(h1T_ready, i)
                    transposes(p_t1, h1, MK, t1_done)
                if is_tile(pair, n - 2, last):
                    e3 = expert(pair, n - 2)
                    pe.wait_ge(h2T_ready, i - 1)
                    if later(pair, n, 3):
                        pe.wait_ge(y_ready, i - 2)
                    product(p_l3, h2T[b], MK, H, e3, W3O // CH, l3_done)

            transpose_rows(0, 0)
            turns(pe, turn)

            pe.wait_ge(amax_ready, 1)
            PE.transpose(p_small[0:1, 0:P], amax1[:, :], ident[:, :]).then_inc(amax_T, 1)
            pe.wait_ge(amax_one, 1)
            PE.matmul(p_small[:, 0:1], ones32[0:1, :], amax_row[:, :], start=True, stop=True).then_inc(amax_all, 1)

            def transpose_group(pair, n):
                g, b = 2 * pair + n, n % 2
                pe.wait_ge(q_ready, g + 1)
                if later(pair, n, 2):
                    pe.wait_ge(qT_ready, g - 1)
                pq = p_qT[b][:, :].bitcast(BF16)
                for j in range(CG * HK):
                    last = PE.transpose(pq[:, j * P:(j + 1) * P], q16[b][:, j * P:(j + 1) * P], ident16[:, :])
                last.then_inc(qT_done, 1)

            def group(pair, n):
                g, b = 2 * pair + n, n % 2
                if is_group(pair, n + 1):
                    transpose_group(pair, n + 1)
                pe.wait_ge(qT_ready, g + 1)
                if later(pair, n, 2):
                    pe.wait_ge(res_ready, g - 1)
                for c in range(CG):
                    for k in range(HK):
                        j = c * HK + k
                        last = PE.matmul(p_out[b][c // 2][:, (c % 2) * H:(c % 2 + 1) * H],
                                         qT[b][:, j * P:(j + 1) * P], fw_q[:, k, :],
                                         start=(k == 0), stop=(k == HK - 1))
                last.then_inc(ffn_done, 1)

            transpose_group(0, 0)
            groups(pe, group)


def kernel(x, cond_256, L0_cond_rms_w, L0_cond_wg_W, L0_cond_wg_b, L0_cond_gg_W, L0_cond_gg_b, L0_cond_W1,
           L0_cond_b1, L0_cond_W2, L0_cond_b2, L0_cond_W3, L0_cond_b3, L0_ffn_weight, L0_ffn_bias):
    import numpy as np
    import concourse.bacc as bacc
    from concourse.bass_utils import run_bass_kernel_spmd

    def np_(a):
        return np.asarray(a)

    x_rows = np_(x).reshape(-1, np_(x).shape[-1])
    E = np_(L0_cond_W1).shape[0]

    def chunks(a):
        a = np_(a)
        return a.reshape(E, a.shape[1] // 128, 128, a.shape[2]).transpose(2, 0, 1, 3).reshape(128, E, -1)

    arrays = {
        "x": x_rows,
        "xT": x_rows.T,
        "condT": np_(cond_256).reshape(-1, 2, np_(cond_256).shape[-1]).transpose(2, 1, 0).reshape(np_(cond_256).shape[-1], -1),
        "rms": np_(L0_cond_rms_w).reshape(-1, 128).T,
        "wg": np_(L0_cond_wg_W), "wgb": np_(L0_cond_wg_b), "gg": np_(L0_cond_gg_W), "ggb": np_(L0_cond_gg_b),
        "w": np.concatenate([chunks(L0_cond_W1), chunks(L0_cond_W2), chunks(L0_cond_W3)], axis=2).reshape(128, -1),
        "b1": np_(L0_cond_b1), "b2": np_(L0_cond_b2), "b3": np_(L0_cond_b3),
        "fwT": np_(L0_ffn_weight).T, "fbias": np_(L0_ffn_bias),
    }
    arrays = {name: np.ascontiguousarray(a) for name, a in arrays.items()}
    nc = bacc.Bacc("TRN2", target_bir_lowering=False, num_devices=1)
    args = {name: nc.dram_tensor(f"in_{name}", a.shape, mybir.dt.from_np(a.dtype), kind="ExternalInput").ap()
            for name, a in arrays.items()}
    out = nc.dram_tensor("out_0", x_rows.shape, F32, kind="ExternalOutput").ap()
    moe_ffn(nc, out=out, **args)
    r = run_bass_kernel_spmd(nc, [{f"in_{name}": a for name, a in arrays.items()}], core_ids=[0])
    return r.results[0]["out_0"].reshape(np_(x).shape)
```

```python
from contextlib import ExitStack

import concourse.bass as bass
from concourse import mybir

P = 128
ALU = mybir.AluOpType
ACT = mybir.ActivationFunctionType
AX = mybir.AxisListType
F32 = mybir.dt.float32
F32R = mybir.dt.float32r
BF16 = mybir.dt.bfloat16
I32 = mybir.dt.int32
U32 = mybir.dt.uint32
MAGIC = 12582912.0


def moe_ffn(nc, x, condT, rms, wg, wgb, gg, ggb, w, b1, b2, b3, fwT, fbias, out):
    T, H = x.shape
    E = wg.shape[1]
    M = b1.shape[1]
    NB = condT.shape[1]
    G = condT.shape[0]
    C = T // P
    HK, MK = H // P, M // P
    WE = HK * M + MK * M + MK * H
    W2O, W3O = HK * M, HK * M + MK * M
    NT = (2 * T + E * (P - 1)) // P
    NT += NT % 2
    FULL = 2 * T // P // 2
    DUMMY = 2 * T
    CW = C * E
    SB = T // NB
    assert C * 2 == NB and SB * 2 == P and HK == 2 and MK == 4

    with ExitStack() as ctx:
        def sb(name, shape, dt=F32):
            return ctx.enter_context(nc.sbuf_tensor(name, shape, dt))

        def sem(name):
            return ctx.enter_context(nc.semaphore(name))

        pair_rows = nc.dram_tensor("pair_rows", [2 * T + 2 * P, H], F32, kind="Internal").ap()

        CH = 512
        EC = WE // CH
        RING = 3
        SLOT = 2 * WE
        ring_at = (nc.sbuf_base + 31) // 32 * 32
        ring = sb("ring", [P, RING * SLOT], F32R)
        stage = sb("stage", [P, 2 * WE])
        slots = [nc.alloc_sbuf_tensor_at(f"slot{n}", [P, SLOT], F32, offset=ring_at + n * SLOT * 4)
                 for n in range(RING)]

        def slot_words(n, words):
            return slots[n][:, 0:words]

        squares = slot_words(0, C * H)
        x_tok = slot_words(1, C * H)
        GC = 4
        TG = GC * P
        x_feat = slot_words(2, 4 * HK * TG).rearrange("p (g k t) -> p g k t", g=4, k=HK)
        gateT = slot_words(2, 4 * HK * TG + T)[0:E, 4 * HK * TG:]
        half = C * P // 2
        onehot_r, onehot_t, is_in_tile = [], [], []
        for k in range(2):
            onehot_r.append(slots[1 + k][:, 0:half].bitcast(BF16).rearrange("p (c r) -> p c r", c=C))
            onehot_t.append(slots[1 + k][:, half:half + C * NT].bitcast(BF16)
                            .rearrange("p (c v t) -> p c v t", c=C, v=2))
            is_in_tile.append(slots[1 + k][:, half + C * NT:half + C * NT + C * NT // 2].bitcast(BF16)
                              .rearrange("p (c t) -> p c t", c=C))
        y_low = slot_words((E - 2) % RING, C * H)
        y_high = slot_words((E - 3) % RING, C * H)
        x_res = slot_words((E - 1) % RING, C * H)

        CG = 4
        NG = C // CG
        scratch = stage[:, WE:WE + 4 * CG * H]
        q16 = [scratch[:, n * CG * H // 2:(n + 1) * CG * H // 2].bitcast(BF16) for n in range(2)]
        qT = [scratch[:, (n + 2) * CG * H // 2:(n + 3) * CG * H // 2].bitcast(BF16) for n in range(2)]
        res = [scratch[:, (n + 2) * CG * H:(n + 3) * CG * H] for n in range(2)]
        taken = [0]

        def tmp(words):
            taken[0] += words
            assert taken[0] <= scratch.shape[1]
            return scratch[:, taken[0] - words:taken[0]]

        take_now = [sb(f"take_now{n}", [P, 1], I32) for n in range(2)]
        put_now = [sb(f"put_now{n}", [P, 1], I32) for n in range(2)]
        rows = [sb(f"rows{n}", [P, H]) for n in range(2)]
        xt = [sb(f"xt_{n}", [P, H], F32R) for n in ("rounded", "rest")]
        h1 = sb("h1", [P, M])
        h2 = sb("h2", [P, M])
        h1T = [[sb(f"h1T{b}_{n}", [P, M], F32R) for n in ("rounded", "rest")] for b in range(2)]
        h2T = [[sb(f"h2T{b}_{n}", [P, M], F32R) for n in ("rounded", "rest")] for b in range(2)]
        small = sb("small", [P, 21 * C])
        gate_in = sb("gate_in", [P, 2 * P])
        y = [sb(f"y{n}", [P, H]) for n in range(2)]

        b1_b = sb("b1_b", [P, E * M])
        b2_b = sb("b2_b", [P, E * M])
        b3_b = sb("b3_b", [P, E * H])
        ident = sb("ident", [P, P])
        ident16 = sb("ident16", [P, P], BF16)
        ones16 = rows[0][:, 0:P // 2].bitcast(BF16)
        ones32 = sb("ones32", [P, P])
        earlier = rows[1][:, 0:P // 2].bitcast(BF16)
        count_r = tmp(P // 2).bitcast(BF16)
        count_t = tmp(NT)
        count_e = y[1][:, 3 * E:4 * E]
        col_no = y[1][:, P:P + 2 * C]
        part_no = sb("part_no", [P, 2])
        dummy_no = tmp(NT)
        batch_half = rows[0][0:NB, P:2 * P]
        batch_col = gate_in[0:NB, P // 2:P // 2 + C]
        rms_sb = y[0][:, 0:HK]
        wg_sb = gate_in[:, 0:HK * E].rearrange("p (k e) -> p k e", k=HK)
        wgf = gate_in[:, HK * E:2 * HK * E].rearrange("p (k e) -> p k e", k=HK)
        condT_sb = gate_in[0:G, P:P + NB]
        gg_sb = y[0][0:G, 1 * E:2 * E]
        wgb_sb = y[0][0:NB, 2 * E:3 * E]
        ggb_sb = y[0][0:NB, 3 * E:4 * E]
        gb = y[0][0:NB, 4 * E:5 * E]
        is_first_sb = sb("is_first_sb", [P, CW])
        gb_col = is_first_sb[0:NB, :]
        sumsq = small[:, 12 * C:13 * C]
        mean_sq = small[:, 13 * C:14 * C]
        root = small[:, 14 * C:15 * C]
        rs = small[:, 15 * C:16 * C]
        tmp_c = small[:, 16 * C:17 * C]
        prob = sb("prob", [P, CW])
        rest = tmp(CW)
        t8 = tmp(CW)
        is_first, is_second = is_first_sb, gate_in
        chosen16 = tmp(CW // 2).bitcast(BF16)
        top = small[:, 17 * C:18 * C]
        first = small[:, 18 * C:19 * C]
        second = small[:, 19 * C:20 * C]
        which = sb("which", [P, 2, C])
        pair_w = sb("pair_w", [P, 2, C])
        tot = tmp(CW)
        seg = tmp(CW)
        incl = tmp(CW)
        n_tiles = y[1][:, 0 * E:1 * E]
        tile_end = y[1][:, 1 * E:2 * E]
        one_e = y[1][:, 2 * E:3 * E]
        slot_at = tmp(CW)
        slot = small[:, 0 * C:2 * C].rearrange("p (k c) -> p k c", k=2)
        slot_t = small[:, 2 * C:4 * C].rearrange("p (k c) -> p k c", k=2)
        slot_r = small[:, 4 * C:6 * C].rearrange("p (k c) -> p k c", k=2)
        past = tmp(NT * (E - 1))
        tile_e = sb("tile_e", [P, NT], I32)
        tile_start = tmp(NT)
        pace = tmp(NT)
        pace_i = sb("pace_i", [P, NT + 1], I32)
        scatters_f = sb("scatters_f", [P, 5])
        scatters = sb("scatters", [P, 5], I32)
        twos = sb("twos", [P, 1], I32)
        tab = tmp(2 * NT)
        tab_k = tmp(NT)
        tab_v = tmp(NT)
        tab_x = tmp(NT)
        tile_x = tmp(NT)
        take_row = sb("take_row", [P, NT + 3], I32)
        put_row = sb("put_row", [P, NT], I32)

        fw_sb = h1
        fw_pos = h2
        fw_q = sb("fw_q", [P, HK, H], BF16)
        fb_b = sb("fb_b", [P, H])
        fsum = sb("fsum", [P, 1])
        w_scale = sb("w_scale", [P, 1])
        thr = sb("thr", [P, 2])
        amax = sb("amax", [P, 4])
        amax1 = sb("amax1", [P, 1])
        amax_row = sb("amax_row", [1, 1])
        i_scale = sb("i_scale", [P, 1])
        i_inv = sb("i_inv", [P, 1])
        out_scale = sb("out_scale", [P, 1])
        magic = sb("magic", [P, 1])

        bank = [ctx.enter_context(nc.psum_tensor(f"bank{n}", [P, 512], F32)) for n in range(8)]
        p_l1, p_l2, p_l3, p_t0, p_t1, p_t2 = bank[:6]
        p_rank, p_total, p_table = bank[0], bank[1], bank[2]
        p_gate, p_small = bank[6], bank[7]
        p_feat = [[bank[0], bank[1]], [bank[2], bank[3]]]
        p_gateT = [bank[4], bank[5]]
        p_qT = [bank[0], bank[1]]
        p_out = [[bank[2], bank[3]], [bank[4], bank[5]]]

        small_in = sem("small_in")
        ffn_in = sem("ffn_in")
        bias_in = sem("bias_in")
        feat_T, feat_copied = sem("feat_T"), sem("feat_copied")
        gateT_done, gateT_copied = sem("gateT_done"), sem("gateT_copied")
        tok_in = [sem(f"tok_in{n}") for n in range(T // TG)]
        expert_in = [sem(f"expert_in{n}") for n in range(2)]
        chunk_in = [sem(f"chunk_in{n}") for n in range(4)]
        slots_ready = sem("slots_ready")
        in_tile_ready = sem("in_tile_ready")
        onehots_c = sem("onehots_c")
        rows_ready = sem("rows_ready")
        raw_ready = sem("raw_ready")
        chunks_rounded = sem("chunks_rounded")
        chunks_done = sem("chunks_done")
        pool_step = sem("pool_step")
        ident_ready, consts_ready = sem("ident_ready"), sem("consts_ready")
        vec_step = sem("vec_step")
        wgf_ready = sem("wgf_ready")
        cond_done = sem("cond_done")
        gb_ready = sem("gb_ready")
        gates_done = sem("gates_done")
        sumsq_done = sem("sumsq_done")
        mean_ready = sem("mean_ready")
        root_ready = sem("root_ready")
        logits_ready = sem("logits_ready")
        exp_done = sem("exp_done")
        chosen_ready = sem("chosen_ready")
        ranks_done = sem("ranks_done")
        onehots_p = sem("onehots_p")
        tables_done = sem("tables_done")
        distances, last_rows = sem("distances"), sem("last_rows")
        tiles_counted = sem("tiles_counted")
        twos_ready = sem("twos_ready")
        take_ready = sem("take_ready")
        paced = sem("paced")
        put_ready = sem("put_ready")
        fsum_ready = sem("fsum_ready")
        fsum_done = sem("fsum_done")
        dma_go = sem("dma_go")
        take_set = sem("take_set")
        put_set = sem("put_set")
        gathered = [sem(f"gathered{n}") for n in range(2)]
        scattered = [sem(f"scattered{n}") for n in range(2)]
        t0_done, xt_ready = sem("t0_done"), sem("xt_ready")
        xt_rounded, h1T_rounded, h2T_rounded = sem("xt_rounded"), sem("h1T_rounded"), sem("h2T_rounded")
        l1_done, h1_ready, t1_done, h1T_ready = sem("l1_done"), sem("h1_ready"), sem("t1_done"), sem("h1T_ready")
        l2_done, h2_ready, t2_done, h2T_ready = sem("l2_done"), sem("h2_ready"), sem("t2_done"), sem("h2T_ready")
        l3_done, y_ready = sem("l3_done"), sem("y_ready")
        low_in = [sem(f"low_in{n}") for n in range(4)]
        high_in = [sem(f"high_in{n}") for n in range(4)]
        res_in = [sem(f"res_in{n}") for n in range(4)]
        low_scaled = sem("low_scaled")
        high_scaled = sem("high_scaled")
        high_summed = sem("high_summed")
        res_biased = sem("res_biased")
        amax_ready, amax_T, amax_one, amax_all = sem("amax_ready"), sem("amax_T"), sem("amax_one"), sem("amax_all")
        clipped = sem("clipped")
        rounded, q_ready, qT_done, qT_ready, ffn_done, res_ready = (
            sem("rounded"), sem("q_ready"), sem("qT_done"), sem("qT_ready"), sem("ffn_done"), sem("res_ready"))
        stored = [sem(f"stored{n}") for n in range(2)]

        PEEL = 4

        def turns(eng, body):
            for i in range(PEEL):
                body(0, i)
            with eng.Fori(0, FULL - PEEL // 2) as pair:
                body(pair, PEEL)
                body(pair, PEEL + 1)
            used = eng.value_load(twos[0:1, 0:1], min_val=0, max_val=NT // 2 - FULL)
            with eng.Fori(0, NT // 2 - FULL) as pair:
                with eng.If(pair < used):
                    body(pair, 2 * FULL)
                    body(pair, 2 * FULL + 1)
            body(used, 2 * FULL, True)
            body(used, 2 * FULL + 1, True)

        def is_tile(pair, n, last=False):
            return n < 2 * FULL if last else not isinstance(pair, int) or n >= 0

        def later(pair, n, first):
            return not isinstance(pair, int) or n >= first

        def groups(eng, body):
            body(0, 0)
            body(0, 1)
            with eng.Fori(0, NG // 2 - 3) as pair:
                body(pair, 2)
                body(pair, 3)
            for n in range(NG - 4, NG):
                body(0, n)

        def is_group(pair, n):
            return not isinstance(pair, int) or n < NG

        block = ctx.enter_context(nc.Block())
        QC = C // 4

        halves = [(k, slice(h * C // 2, (h + 1) * C // 2)) for k in range(2) for h in range(2)]

        def quarter(ap, n):
            return ap[:, n * QC * H:(n + 1) * QC * H].rearrange("p (c h) -> p c h", c=QC)

        def token_rows(dram, first_row, n):
            return dram[first_row + n * QC * P:first_row + (n + 1) * QC * P, :].rearrange("(c p) h -> p c h", p=P)

        @block.sync
        def _(sp):
            def load_tokens(g):
                sp.dma_start(x_tok[:, g * GC * H:(g + 1) * GC * H].rearrange("p (c h) -> p c h", c=GC),
                             x[g * TG:(g + 1) * TG, :].rearrange("(c p) h -> p c h", p=P)).then_inc(tok_in[g], 16)

            load_tokens(0)
            load_tokens(1)
            for dst, src in ((rms_sb[:, :], rms), (wg_sb[:, :, :], wg.rearrange("(k p) e -> p k e", p=P)),
                             (condT_sb[:, :], condT), (gg_sb[:, :], gg), (wgb_sb[:, :], wgb.partition_broadcast(NB)),
                             (ggb_sb[:, :], ggb.partition_broadcast(NB))):
                sp.dma_start(dst, src).then_inc(small_in, 16)
            for g in range(2, T // TG):
                load_tokens(g)
            def load_expert(e):
                sp.dma_start(stage[:, e * WE:(e + 1) * WE], w[:, e * WE:(e + 1) * WE]).then_inc(expert_in[e], 16)
                sp.wait_ge(expert_in[e], 16)
                sp.sem_inc(raw_ready, EC)

            def load_chunk(chunk, n):
                sp.wait_ge(chunks_done, chunk - (2 * EC - 1))
                sp.dma_start(stage[:, bass.ds(chunk % (2 * EC) * CH, CH)], w[:, bass.ds(chunk * CH, CH)]
                             ).then_inc(chunk_in[n], 16)

            load_expert(0)
            sp.wait_ge(put_ready, 1)
            sp.wait_ge(gathered[1], 16)
            load_expert(1)
            for n in range(4):
                load_chunk(2 * EC + n, n)
            with sp.Fori(1, (E - 2) * EC // 4) as four:
                for n in range(4):
                    sp.wait_ge(chunk_in[n], four * 16)
                    sp.sem_inc(raw_ready, 1)
                    load_chunk(four * 4 + (2 * EC + n), n)
            for n in range(4):
                sp.wait_ge(chunk_in[n], (E - 2) * EC // 4 * 16)
                sp.sem_inc(raw_ready, 1)

            def wait_scatters(col):
                rows_done = sp.value_load(scatters[0:1, col:col + 1], min_val=16, max_val=8 * NT)
                sp.wait_ge(scattered[0], rows_done)
                sp.wait_ge(scattered[1], rows_done)

            wait_scatters(0)
            for n in range(4):
                sp.dma_start(quarter(y_low, n), token_rows(pair_rows, 0, n)).then_inc(low_in[n], 16)
                sp.wait_ge(low_in[n], 16)
            for n in range(4):
                wait_scatters(2 + n if n < 3 else 1)
                sp.dma_start(quarter(y_high, n), token_rows(pair_rows, T, n)).then_inc(high_in[n], 16)
            for n in range(4):
                sp.dma_start(quarter(x_res, n), token_rows(x, 0, n)).then_inc(res_in[n], 16)
            out_v = out.rearrange("(g c p) h -> p g c h", p=P, c=CG)
            with sp.Fori(0, NG // 2) as turn:
                for n in range(2):
                    sp.wait_ge(res_ready, 2 * turn + n + 1)
                    sp.dma_start(out_v[:, bass.ds(2 * turn + n, 1), :, :].rearrange("p g c h -> p (g c) h"),
                                 res[n][:, :].rearrange("p (c h) -> p c h", c=CG)).then_inc(stored[n], 16)
            for n in range(2):
                sp.wait_ge(stored[n], 16 * (NG // 2))

        @block.gpsimd
        def _(pool):
            steps = [0]

            def step(ins):
                steps[0] += 1
                ins.then_inc(pool_step, 1)
                pool.wait_ge(pool_step, steps[0])

            def one_on_diagonal(m):
                step(nc.gpsimd.affine_select(out=m[:, :], in_=m[:, :], compare_op=ALU.not_equal, fill=1.0, base=0,
                                             pattern=[[-1, P]], channel_multiplier=1))

            step(nc.gpsimd.memset(ident[:, :], 0.0))
            one_on_diagonal(ident)
            pool.sem_inc(ident_ready, 1)
            for dst, value in ((ident16, 0.0), (earlier, 1.0), (batch_half, 0.0), (batch_col, 0.0),
                               (ones16, 1.0), (ones32, 1.0)):
                step(nc.gpsimd.memset(dst[:, :], value))
            one_on_diagonal(ident16)
            step(nc.gpsimd.affine_select(out=earlier[:, :], in_=earlier[:, :], compare_op=ALU.is_gt, fill=0.0, base=0,
                                         pattern=[[1, P]], channel_multiplier=-1))
            step(nc.gpsimd.memset(batch_half[0:C, 0:SB], 1.0))
            step(nc.gpsimd.memset(batch_half[C:2 * C, SB:P], 1.0))
            for h in range(2):
                step(nc.gpsimd.affine_select(out=batch_col[:, :], in_=batch_col[:, :], compare_op=ALU.not_equal,
                                             fill=1.0, base=-h * C, pattern=[[-1, C]], channel_multiplier=1))

            def count(out_ap, pattern, base=0, mult=0):
                return nc.gpsimd.iota(out_ap, pattern=pattern, base=base, channel_multiplier=mult,
                                      allow_small_or_imprecise_dtypes=True)

            step(count(count_r[:, :], [[1, P]]))
            step(count(count_t[:, :], [[1, NT]]))
            step(count(count_e[:, :], [[1, E]], base=-E))
            step(count(col_no[:, :].rearrange("p (k c) -> p k c", k=2), [[-1, 2], [1, C]], base=1))
            step(count(part_no[:, :], [[P, 2]], mult=1))
            step(count(dummy_no[:, :].rearrange("p (a b) -> p a b", b=2), [[0, NT // 2], [P, 2]],
                       base=DUMMY + P, mult=1))
            pool.sem_inc(consts_ready, 1)

            def split(chunk):
                at = chunk % (RING * EC) * (2 * CH)
                nc.gpsimd.tensor_tensor(ring[:, bass.ds(at + CH, CH)], stage[:, bass.ds(chunk % (2 * EC) * CH, CH)],
                                        ring[:, bass.ds(at, CH)].bitcast(F32), ALU.subtract).then_inc(chunks_done, 1)

            pool.wait_ge(chunks_rounded, EC)
            for chunk in range(EC):
                split(chunk)

            for n, (k, part) in enumerate(halves):
                pool.wait_ge(in_tile_ready, n + 1)
                nc.gpsimd.tensor_tensor(onehot_t[k][:, part, 0, :], is_in_tile[k][:, part, :],
                                        col_no[:, k * C + part.start:k * C + part.stop].unsqueeze(2)
                                        .to_broadcast([P, C // 2, NT]), ALU.mult).then_inc(onehots_c, 1)

            pool.wait_ge(tiles_counted, 1)
            quarters = incl[:, (E - 1) * C:E * C].rearrange("p (q c) -> p q c", c=QC)[:, 0:3, QC - 1]
            step(nc.gpsimd.tensor_scalar(scatters_f[:, 2:5], quarters, 1.0 / P, 0.5 - 0.5 / P, ALU.mult, ALU.add))
            step(nc.gpsimd.tensor_scalar(scatters_f[:, 2:5], scatters_f[:, 2:5], MAGIC, MAGIC, ALU.add, ALU.subtract))
            step(nc.gpsimd.tensor_tensor(scatters_f[:, 2:5], scatters_f[:, 2:5],
                                         tile_end[:, E - 2:E - 1].to_broadcast([P, 3]), ALU.add))
            step(nc.gpsimd.tensor_scalar(scatters_f[:, 0:2], tile_end[:, E - 2:E], 1.0, None, ALU.mult))
            step(nc.gpsimd.tensor_scalar(scatters_f[:, :], scatters_f[:, :], 0.5, 0.25, ALU.mult, ALU.add))
            step(nc.gpsimd.tensor_scalar(scatters_f[:, :], scatters_f[:, :], MAGIC, MAGIC, ALU.add, ALU.subtract))
            step(nc.gpsimd.tensor_scalar(scatters[:, :], scatters_f[:, :], 16.0, None, ALU.mult))
            step(nc.gpsimd.tensor_scalar(twos[:, :], scatters_f[:, 1:2], -float(FULL), None, ALU.add))
            pool.sem_inc(twos_ready, 1)

            pool.wait_ge(take_ready, 1)

            def gather(pair, n):
                i, b = 2 * pair + n, n % 2
                if later(pair, n, 2):
                    pool.wait_ge(t0_done, i - 1)
                nc.gpsimd.tensor_copy(take_now[b][:, :], take_row[:, bass.ds(i, 1)]).then_inc(take_set, 1)
                pool.wait_ge(take_set, i + 1)
                pool.sem_inc(dma_go, 1)
                nc.gpsimd.indirect_dma_start(
                    rows[b][:, :], None, x, bass.IndirectOffsetOnAxis(ap=take_now[b][:, 0:1].bitcast(U32), axis=0)
                ).then_inc(gathered[b], 16)

            def scatter(pair, n):
                i, b = 2 * pair + n, n % 2
                if later(pair, n, 2):
                    pool.wait_ge(scattered[b], 16 * (pair + n // 2))
                nc.gpsimd.tensor_copy(put_now[b][:, :], put_row[:, bass.ds(i, 1)]).then_inc(put_set, 1)
                pool.wait_ge(put_set, i + 1)
                pool.wait_ge(y_ready, i + 1)
                pool.sem_inc(dma_go, 1)
                nc.gpsimd.indirect_dma_start(
                    pair_rows, bass.IndirectOffsetOnAxis(ap=put_now[b][:, 0:1].bitcast(U32), axis=0), y[b][:, :], None
                ).then_inc(scattered[b], 16)

            for i in range(3):
                gather(0, i)
            pool.wait_ge(paced, 1)
            pool.wait_ge(put_ready, 1)

            def split_some(pair, n):
                i = 2 * pair + n
                done = pool.value_load(pace_i[0:1, bass.ds(i, 1)], min_val=0, max_val=EC * E)
                goal = pool.value_load(pace_i[0:1, bass.ds(i + 1, 1)], min_val=0, max_val=EC * E)
                with pool.If(done < goal):
                    with pool.Fori(done, goal) as chunk:
                        pool.wait_ge(chunks_rounded, chunk + 1)
                        split(chunk)

            def turn(pair, n, last=False):
                if is_tile(pair, n + 3, last):
                    gather(pair, n + 3)
                if is_tile(pair, n - 2, last):
                    scatter(pair, n - 2)
                if is_tile(pair, n, last):
                    split_some(pair, n)

            turns(pool, turn)

            pool.wait_ge(ffn_in, 32)
            xr = x_res.rearrange("p (c h) -> p c h", c=C)

            def bias_quarter(n):
                pool.wait_ge(res_in[n], 16)
                part = xr[:, n * QC:(n + 1) * QC, :]
                nc.gpsimd.tensor_tensor(part, part, fb_b[:, :].unsqueeze(1).to_broadcast([P, QC, H]),
                                        ALU.add).then_inc(res_biased, 1)

            pool.wait_ge(low_scaled, 4)
            pool.wait_ge(high_scaled, 1)
            last = slice(3 * QC * H, C * H)
            nc.gpsimd.tensor_tensor(y_high[:, last], y_high[:, last], y_low[:, last], ALU.add).then_inc(high_summed, 1)
            for n in range(4):
                bias_quarter(n)

        @block.scalar
        def _(act):
            act.dma_start(fw_sb[:, :].rearrange("p (k o) -> p k o", k=HK),
                          fwT.rearrange("(k p) o -> p k o", p=P)).then_inc(ffn_in, 16)
            act.dma_start(fb_b[:, :], fbias.partition_broadcast(P)).then_inc(ffn_in, 16)
            for g in range(T // TG):
                act.wait_ge(tok_in[g], 16)
                for c in range(g * GC, (g + 1) * GC):
                    col = slice(c * H, (c + 1) * H)
                    last = nc.scalar.activation(squares[:, col], x_tok[:, col], ACT.Square, accum_out=sumsq[:, c:c + 1])
            last.then_inc(sumsq_done, 1)
            for dst, src in ((b1_b, b1), (b2_b, b2), (b3_b, b3)):
                act.dma_start(dst[:, :], src.rearrange("e m -> (e m)").partition_broadcast(P)).then_inc(bias_in, 16)

            def round_chunk(chunk):
                nc.scalar.activation(ring[:, bass.ds(chunk % (RING * EC) * (2 * CH), CH)],
                                     stage[:, bass.ds(chunk % (2 * EC) * CH, CH)], ACT.Copy).then_inc(chunks_rounded, 1)

            act.wait_ge(mean_ready, 1)
            nc.scalar.activation(root[:, :], mean_sq[:, :], ACT.Sqrt).then_inc(root_ready, 1)
            act.wait_ge(sumsq_done, 1)
            act.wait_ge(raw_ready, EC)
            for chunk in range(EC):
                round_chunk(chunk)
            act.wait_ge(slots_ready, 1)
            last_k, last_part = halves[-1]

            def distances_of(first, count):
                for c in range(last_part.start + first, last_part.start + first + count):
                    last = nc.scalar.activation(onehot_r[last_k][:, c, :], count_r[:, :], ACT.Square, scale=-1.0,
                                                bias=slot_r[:, last_k, c:c + 1])
                last.then_inc(distances, 1)

            def tiles_times_partition(n):
                k, part = halves[n]
                act.wait_ge(in_tile_ready, n + 1)
                nc.scalar.activation(onehot_t[k][:, part, 1, :], is_in_tile[k][:, part, :], ACT.Copy,
                                     scale=part_no[:, k:k + 1]).then_inc(onehots_p, 1)

            distances_of(0, 6)
            tiles_times_partition(0)
            distances_of(6, 8)
            tiles_times_partition(1)
            distances_of(14, C // 2 - 14)
            act.wait_ge(distances, 3)
            last_rows_at = onehot_r[last_k][:, last_part, :]
            nc.scalar.activation(last_rows_at, last_rows_at, ACT.Relu, scale=-1.0, bias=one_e[:, 0:1]
                                 ).then_inc(last_rows, 1)
            tiles_times_partition(2)
            tiles_times_partition(3)
            act.wait_ge(logits_ready, 1)
            nc.scalar.activation(prob[:, :], prob[:, :], ACT.Exp).then_inc(exp_done, 1)

            def turn(pair, n, last=False):
                i, b = 2 * pair + n, n % 2
                if is_tile(pair, n - 2, last):
                    act.wait_ge(t2_done, i - 1)
                    if later(pair, n, 4):
                        act.wait_ge(l3_done, i - 3)
                    nc.scalar.activation(h2T[b][0][:, :], p_t2[:, :], ACT.Relu).then_inc(h2T_rounded, 1)
                if is_tile(pair, n + 1, last):
                    act.wait_ge(t0_done, i + 2)
                    nc.scalar.activation(xt[0][:, :], p_t0[:, 0:H], ACT.Copy).then_inc(xt_rounded, 1)
                if is_tile(pair, n, last):
                    act.wait_ge(t1_done, i + 1)
                    if later(pair, n, 2):
                        act.wait_ge(l2_done, i - 1)
                    nc.scalar.activation(h1T[b][0][:, :], p_t1[:, :], ACT.Relu).then_inc(h1T_rounded, 1)
                    done = act.value_load(pace_i[0:1, bass.ds(i, 1)], min_val=0, max_val=EC * E)
                    goal = act.value_load(pace_i[0:1, bass.ds(i + 1, 1)], min_val=0, max_val=EC * E)
                    with act.If(done < goal):
                        if later(pair, n, 2):
                            act.wait_ge(l3_done, i - 1)
                        with act.Fori(done, goal) as chunk:
                            act.wait_ge(raw_ready, chunk + 1)
                            round_chunk(chunk)

            act.wait_ge(paced, 1)
            act.wait_ge(t0_done, 1)
            nc.scalar.activation(xt[0][:, :], p_t0[:, 0:H], ACT.Copy).then_inc(xt_rounded, 1)
            turns(act, turn)

            for n in range(4):
                act.wait_ge(low_in[n], 16)
                for c in range(n * QC, (n + 1) * QC):
                    part = y_low[:, c * H:(c + 1) * H]
                    last = nc.scalar.activation(part, part, ACT.Copy, scale=pair_w[:, 0, c:c + 1])
                last.then_inc(low_scaled, 1)
            act.wait_ge(high_in[3], 16)
            for c in range(3 * QC, C):
                part = y_high[:, c * H:(c + 1) * H]
                last = nc.scalar.activation(part, part, ACT.Copy, scale=pair_w[:, 1, c:c + 1])
            last.then_inc(high_scaled, 1)

            def integers(pair, n):
                g, b = 2 * pair + n, n % 2
                act.wait_ge(clipped, g + 1)
                if later(pair, n, 2):
                    act.wait_ge(qT_done, g - 1)
                nc.scalar.activation(q16[b][:, :], y_high[:, bass.ds(g * CG * H, CG * H)], ACT.Identity,
                                     bias=magic[:, 0:1]).then_inc(q_ready, 1)

            def group(pair, n):
                g, b = 2 * pair + n, n % 2
                if is_group(pair, n + 1):
                    integers(pair, n + 1)
                act.wait_ge(qT_done, g + 1)
                if later(pair, n, 2):
                    act.wait_ge(ffn_done, g - 1)
                nc.scalar.activation(qT[b][:, :], p_qT[b][:, :].bitcast(BF16), ACT.Copy).then_inc(qT_ready, 1)

            integers(0, 0)
            groups(act, group)

        @block.vector
        def _(dve):
            steps = [0]
            V = nc.vector

            def step(ins):
                steps[0] += 1
                ins.then_inc(vec_step, 1)
                dve.wait_ge(vec_step, steps[0])

            def by_ce(ap):
                return ap.rearrange("p (c e) -> p c e", e=E)

            def over_e(ap):
                return ap.unsqueeze(2).to_broadcast([P, C, E])

            e_of = count_e[:, :].unsqueeze(1).to_broadcast([P, C, E])

            step(V.memset(magic[:, :], -MAGIC))
            step(V.memset(one_e[:, :], 1.0))
            step(V.memset(seg[:, :], 1.0))
            step(V.memset(seg[:, :].rearrange("p (e c) -> p e c", e=E)[:, :, 0:1], 0.0))

            def router_weights():
                dve.wait_ge(small_in, 16 * 6)
                for k in range(HK):
                    step(V.tensor_scalar(wgf[:, k, :], wg_sb[:, k, :], rms_sb[:, k:k + 1], None, ALU.mult))
                dve.sem_inc(wgf_ready, 1)
                dve.wait_ge(cond_done, 1)
                dve.wait_ge(consts_ready, 1)
                step(V.tensor_tensor(gb[:, :], p_small[0:NB, 0:E], wgb_sb[:, :], ALU.add))
                step(V.tensor_tensor(gb[:, :], gb[:, :], ggb_sb[:, :], ALU.add))
                V.tensor_tensor(gb_col[:, :].rearrange("p (c e) -> p c e", e=E),
                                gb[:, :].unsqueeze(1).to_broadcast([NB, C, E]),
                                batch_col[:, :].unsqueeze(2).to_broadcast([NB, C, E]), ALU.mult).then_inc(gb_ready, 1)
                dve.wait_ge(ffn_in, 32)
                V.tensor_reduce(fsum[:, :], fw_sb[:, :], AX.X, ALU.add, apply_absolute_value=True
                                ).then_inc(fsum_ready, 1)

            def copy_gates(g):
                dve.wait_ge(gateT_done, g + 1)
                V.tensor_copy(gateT[:, g * TG:(g + 1) * TG], p_gateT[g % 2][0:E, :]).then_inc(gateT_copied, 1)

            for g in range(T // TG):
                for k in range(HK):
                    dve.wait_ge(feat_T, HK * g + k + 1)
                    if g >= 4:
                        dve.wait_ge(gateT_done, g - 3)
                    V.tensor_copy(x_feat[:, g % 4, k, :], p_feat[g % 2][k][:, :]).then_inc(feat_copied, 1)
                if g >= 2:
                    copy_gates(g - 2)
                if g == 1:
                    router_weights()
                elif g == 3:
                    dve.wait_ge(fsum_done, 1)
                    step(V.tensor_scalar(w_scale[:, :], p_small[:, 16:17], 1.0 / (H * H), None, ALU.mult))
                    step(V.tensor_scalar(thr[:, 0:1], w_scale[:, :], 0.5, None, ALU.mult))
                    step(V.tensor_scalar(thr[:, 1:2], w_scale[:, :], -0.5, None, ALU.mult))
                    dve.wait_ge(sumsq_done, 1)
                    V.tensor_scalar(mean_sq[:, :], sumsq[:, :], 1.0 / H, 1e-6, ALU.mult, ALU.add
                                    ).then_inc(mean_ready, 1)
                elif g == 4:
                    step(V.tensor_scalar(fw_pos[:, :], fw_sb[:, :], thr[:, 0:1], None, ALU.is_gt))
                    step(V.scalar_tensor_tensor(fw_pos[:, :], fw_sb[:, :], thr[:, 1:2], fw_pos[:, :],
                                                ALU.is_lt, ALU.subtract))
                elif g == 5:
                    step(V.tensor_scalar(fw_q[:, :, :].rearrange("p k o -> p (k o)"), fw_pos[:, :], -1.0, None,
                                         ALU.mult))
                elif g == 6:
                    dve.wait_ge(root_ready, 1)
                    step(V.reciprocal(rs[:, :], root[:, :]))
                    step(V.tensor_tensor(tmp_c[:, :], rs[:, :], rs[:, :], ALU.mult))
                elif g == 7:
                    step(V.tensor_tensor(tmp_c[:, :], tmp_c[:, :], mean_sq[:, :], ALU.mult))
                    step(V.tensor_scalar(tmp_c[:, :], tmp_c[:, :], -0.5, 1.5, ALU.mult, ALU.add))
                    step(V.tensor_tensor(rs[:, :], rs[:, :], tmp_c[:, :], ALU.mult))
            copy_gates(T // TG - 2)
            copy_gates(T // TG - 1)

            dve.wait_ge(gates_done, 1)
            step(V.tensor_tensor(by_ce(prob[:, :]), by_ce(p_gate[:, 0:CW]), over_e(rs[:, :]), ALU.mult))
            step(V.tensor_tensor(prob[:, :], prob[:, :], p_gate[:, CW:2 * CW], ALU.add))

            def largest(values, peak, number, onehot):
                step(V.tensor_reduce(peak[:, :], by_ce(values[:, :]), AX.X, ALU.max))
                step(V.tensor_tensor(by_ce(t8[:, :]), by_ce(values[:, :]), over_e(peak[:, :]), ALU.is_equal))
                step(V.tensor_tensor(by_ce(t8[:, :]), by_ce(t8[:, :]), e_of, ALU.mult))
                step(V.tensor_reduce(number[:, :], by_ce(t8[:, :]), AX.X, ALU.min))
                step(V.tensor_tensor(by_ce(onehot[:, :]), e_of, over_e(number[:, :]), ALU.is_equal))

            largest(prob, top, first, is_first)
            step(V.scalar_tensor_tensor(rest[:, :], is_first[:, :], -3e38, prob[:, :], ALU.mult, ALU.add))
            largest(rest, tmp_c, second, is_second)
            V.tensor_tensor(chosen16[:, :], is_first[:, :], is_second[:, :], ALU.add).then_inc(chosen_ready, 1)
            step(V.tensor_tensor(which[:, 0, :], first[:, :], second[:, :], ALU.min))
            step(V.tensor_tensor(which[:, 1, :], first[:, :], second[:, :], ALU.max))
            step(V.tensor_tensor(by_ce(is_first[:, :]), e_of, over_e(which[:, 0, :]), ALU.is_equal))
            step(V.tensor_tensor(by_ce(is_second[:, :]), e_of, over_e(which[:, 1, :]), ALU.is_equal))

            def pick(dst, onehot, values, product=t8):
                step(V.tensor_tensor(product[:, :], onehot[:, :], values[:, :], ALU.mult))
                step(V.tensor_reduce(dst, by_ce(product[:, :]), AX.X, ALU.add))

            dve.wait_ge(ranks_done, 1)
            step(V.tensor_copy(tot[:, :].rearrange("p (e c) -> p e c", e=E),
                               p_total[:, 0:CW].rearrange("p (c e) -> p e c", e=E)))
            step(V.tensor_tensor_scan(incl[:, :], seg[:, :], tot[:, :], 0.0, ALU.mult, ALU.add))
            in_expert = incl[:, :].rearrange("p (e c) -> p e c", e=E)
            step(V.tensor_scalar(n_tiles[:, :].unsqueeze(2), in_expert[:, :, C - 1:C], 1.0 / P, 0.5 - 0.5 / P,
                                 ALU.mult, ALU.add))
            step(V.tensor_scalar(n_tiles[:, :], n_tiles[:, :], MAGIC, MAGIC, ALU.add, ALU.subtract))
            step(V.tensor_scalar(n_tiles[:, :], n_tiles[:, :], 1.0, None, ALU.max))
            step(V.tensor_tensor_scan(tile_end[:, :], one_e[:, :], n_tiles[:, :], 0.0, ALU.mult, ALU.add))
            dve.sem_inc(tiles_counted, 1)
            step(V.tensor_tensor(n_tiles[:, :], tile_end[:, :], n_tiles[:, :], ALU.subtract))
            step(V.tensor_tensor(tot[:, :], incl[:, :], tot[:, :], ALU.subtract))
            step(V.tensor_tensor(by_ce(slot_at[:, :]), by_ce(p_rank[:, 0:CW]),
                                 tot[:, :].rearrange("p (e c) -> p c e", e=E), ALU.add))
            step(V.scalar_tensor_tensor(by_ce(slot_at[:, :]), n_tiles[:, :].unsqueeze(1).to_broadcast([P, C, E]),
                                        float(P), by_ce(slot_at[:, :]), ALU.mult, ALU.add))
            pick(slot[:, 0, :], is_first, slot_at)
            pick(slot[:, 1, :], is_second, slot_at)
            step(V.tensor_scalar(slot_t[:, :, :], slot[:, :, :], 1.0 / P, 0.5 / P - 0.5, ALU.mult, ALU.add))
            step(V.tensor_scalar(slot_t[:, :, :], slot_t[:, :, :], MAGIC, MAGIC, ALU.add, ALU.subtract))
            V.scalar_tensor_tensor(slot_r[:, :, :], slot_t[:, :, :], -float(P), slot[:, :, :], ALU.mult, ALU.add
                                   ).then_inc(slots_ready, 1)
            dve.wait_ge(slots_ready, 1)

            V.tensor_tensor(by_ce(prob[:, :]), by_ce(prob[:, :]), over_e(top[:, :]), ALU.subtract
                            ).then_inc(logits_ready, 1)

            def tiles_of(k, part):
                V.tensor_tensor(is_in_tile[k][:, part, :], slot_t[:, k, part].unsqueeze(2).to_broadcast([P, C // 2, NT]),
                                count_t[:, :].unsqueeze(1).to_broadcast([P, C // 2, NT]), ALU.is_equal
                                ).then_inc(in_tile_ready, 1)

            for n, (k, part) in enumerate(halves):
                if n < 3:
                    tiles_of(k, part)
                if n == 2:
                    tiles_of(*halves[3])
                if n < 3:
                    V.tensor_tensor(onehot_r[k][:, part, :], slot_r[:, k, part].unsqueeze(2).to_broadcast([P, C // 2, P]),
                                    count_r[:, :].unsqueeze(1).to_broadcast([P, C // 2, P]), ALU.is_equal
                                    ).then_inc(rows_ready, 1)

            past_te = past[:, :].rearrange("p (t e) -> p t e", t=NT)
            ends = tile_end[:, 0:E - 1].unsqueeze(1).to_broadcast([P, NT, E - 1])
            step(V.tensor_tensor(past_te, count_t[:, :].unsqueeze(2).to_broadcast([P, NT, E - 1]), ends, ALU.is_ge))
            step(V.tensor_reduce(tile_x[:, :], past_te, AX.X, ALU.add))
            V.tensor_copy(tile_e[:, :], tile_x[:, :])
            V.memset(take_row[:, NT:NT + 3], 0)

            dve.wait_ge(tables_done, 1)
            a, b_ = tab[:, 0:NT], tab[:, NT:2 * NT]
            step(V.tensor_copy(tab[:, :], p_table[:, 0:2 * NT]))
            step(V.scalar_tensor_tensor(tab_x[:, :], a, float(P), b_, ALU.mult, ALU.add))
            step(V.tensor_scalar(take_row[:, 0:NT], tab_x[:, :], -float(P), 0.0, ALU.add, ALU.max))
            dve.sem_inc(take_ready, 1)
            step(V.tensor_tensor(past_te, past_te, ends, ALU.mult))
            step(V.tensor_reduce(tile_start[:, :], past_te, AX.X, ALU.max))
            step(V.tensor_tensor(pace[:, :], count_t[:, :], tile_start[:, :], ALU.subtract))
            step(V.tensor_scalar(pace[:, :], pace[:, :], 2.0, float(EC), ALU.mult, ALU.min))
            step(V.tensor_scalar(tile_x[:, :], tile_x[:, :], float(EC), float(EC), ALU.mult, ALU.add))
            step(V.tensor_tensor(pace[:, :], pace[:, :], tile_x[:, :], ALU.add))
            step(V.tensor_tensor(pace[:, 0:NT - 1], pace[:, 0:NT - 1], tile_x[:, 1:NT], ALU.max))
            V.memset(pace_i[:, 0:1], EC)
            step(V.tensor_scalar(pace_i[:, 1:NT + 1], pace[:, :], float(EC * E), None, ALU.min))
            dve.sem_inc(paced, 1)

            def results_rows():
                step(V.scalar_tensor_tensor(tab_v[:, :], tab_x[:, :], P - 0.5, dummy_no[:, :], ALU.is_lt, ALU.mult))
                step(V.tensor_tensor(tab_x[:, :], tab_x[:, :], tab_v[:, :], ALU.add))
                step(V.tensor_scalar(tab_k[:, :], b_, P - 0.5, float(T), ALU.is_gt, ALU.mult))
                step(V.scalar_tensor_tensor(put_row[:, :], tab_k[:, :], -float(P), tab_x[:, :], ALU.add, ALU.add))
                dve.sem_inc(put_ready, 1)

            def weights_of_pairs(part):
                if part == 0:
                    dve.wait_ge(exp_done, 1)
                    step(V.tensor_reduce(top[:, :], by_ce(prob[:, :]), AX.X, ALU.add))
                    step(V.reciprocal(top[:, :], top[:, :]))
                    step(V.tensor_tensor(by_ce(prob[:, :]), by_ce(prob[:, :]), over_e(top[:, :]), ALU.mult))
                elif part == 1:
                    pick(pair_w[:, 0, :], is_first, prob, is_first)
                elif part == 2:
                    pick(pair_w[:, 1, :], is_second, prob, is_second)

            dve.wait_ge(twos_ready, 1)
            dve.wait_ge(bias_in, 48)

            def expert(pair, n):
                return dve.value_load(tile_e[0:1, bass.ds(2 * pair + n, 1)], min_val=0, max_val=E - 1)

            def rest_of(dst, psum, ready, relu):
                if relu:
                    V.scalar_tensor_tensor(dst[1][:, :], psum, 0.0, dst[0][:, :].bitcast(F32),
                                           ALU.max, ALU.subtract).then_inc(ready, 1)
                else:
                    V.tensor_tensor(dst[1][:, :], psum, dst[0][:, :].bitcast(F32), ALU.subtract).then_inc(ready, 1)

            def turn(pair, n, last=False):
                i, b = 2 * pair + n, n % 2
                if is_tile(pair, n, last):
                    e = expert(pair, n)
                    dve.wait_ge(l1_done, i + 1)
                    if later(pair, n, 1):
                        dve.wait_ge(t1_done, i)
                    V.tensor_tensor(h1[:, :], p_l1[:, :], b1_b[:, bass.ds(e * M, M)],
                                    ALU.add).then_inc(h1_ready, 1)
                if is_tile(pair, n - 2, last):
                    dve.wait_ge(h2T_rounded, i - 1)
                    rest_of(h2T[b], p_t2[:, :], h2T_ready, True)
                if is_tile(pair, n + 1, last):
                    dve.wait_ge(xt_rounded, i + 2)
                    rest_of(xt, p_t0[:, 0:H], xt_ready, False)
                if is_tile(pair, n - 1, last):
                    e = expert(pair, n - 1)
                    dve.wait_ge(l2_done, i)
                    if later(pair, n, 2):
                        dve.wait_ge(t2_done, i - 1)
                    V.tensor_tensor(h2[:, :], p_l2[:, :], b2_b[:, bass.ds(e * M, M)],
                                    ALU.add).then_inc(h2_ready, 1)
                if is_tile(pair, n, last):
                    dve.wait_ge(h1T_rounded, i + 1)
                    rest_of(h1T[b], p_t1[:, :], h1T_ready, True)
                if is_tile(pair, n - 2, last):
                    e = expert(pair, n - 2)
                    dve.wait_ge(l3_done, i - 1)
                    if later(pair, n, 4):
                        dve.wait_ge(scattered[b], 16 * (pair + (n - 2) // 2))
                    V.tensor_tensor(y[b][:, :], p_l3[:, 0:H], b3_b[:, bass.ds(e * H, H)],
                                    ALU.add).then_inc(y_ready, 1)
                if isinstance(pair, int):
                    weights_of_pairs(n - 1)

            dve.wait_ge(xt_rounded, 1)
            rest_of(xt, p_t0[:, 0:H], xt_ready, False)
            results_rows()
            turns(dve, turn)

            for n in range(4):
                part = slice(n * QC * H, (n + 1) * QC * H)
                if n < 3:
                    dve.wait_ge(high_in[n], 16)
                    dve.wait_ge(low_scaled, n + 1)
                    for c in range(n * QC, (n + 1) * QC):
                        col = slice(c * H, (c + 1) * H)
                        last = V.scalar_tensor_tensor(y_high[:, col], y_high[:, col], pair_w[:, 1, c:c + 1],
                                                      y_low[:, col], ALU.mult, ALU.add)
                    step(last)
                else:
                    dve.wait_ge(high_summed, 1)
                step(V.tensor_reduce(amax[:, n:n + 1], y_high[:, part], AX.X, ALU.max, apply_absolute_value=True))
            V.tensor_reduce(amax1[:, :], amax[:, :], AX.X, ALU.max).then_inc(amax_ready, 1)
            dve.wait_ge(amax_T, 1)
            V.tensor_reduce(amax_row[:, :], p_small[0:1, 0:P], AX.X, ALU.max).then_inc(amax_one, 1)
            dve.wait_ge(amax_all, 1)
            step(V.tensor_scalar(i_scale[:, :], p_small[:, 0:1], 1.0 / 127.0, None, ALU.mult))
            step(V.reciprocal(i_inv[:, :], i_scale[:, :]))
            step(V.tensor_tensor(out_scale[:, :], w_scale[:, :], i_scale[:, :], ALU.mult))

            AHEAD = 4

            def scale(pair, n):
                part = y_high[:, bass.ds((2 * pair + n) * CG * H, CG * H)]
                V.tensor_scalar(part, part, i_inv[:, 0:1], MAGIC, ALU.mult, ALU.add).then_inc(rounded, 1)

            def clip(pair, n):
                part = y_high[:, bass.ds((2 * pair + n) * CG * H, CG * H)]
                dve.wait_ge(rounded, 2 * pair + n + 1)
                V.tensor_scalar(part, part, MAGIC - 128.0, MAGIC + 127.0, ALU.max, ALU.min).then_inc(clipped, 1)

            def group(pair, n):
                g, b = 2 * pair + n, n % 2
                if is_group(pair, n + AHEAD):
                    scale(pair, n + AHEAD)
                dve.wait_ge(ffn_done, g + 1)
                dve.wait_ge(res_biased, pair + n // 2 + 1)
                if later(pair, n, 2):
                    dve.wait_ge(stored[b], 16 * (pair + n // 2))
                for h in range(2):
                    last = V.scalar_tensor_tensor(
                        res[b][:, h * 2 * H:(h + 1) * 2 * H], p_out[b][h][:, :], out_scale[:, 0:1],
                        x_res[:, bass.ds(g * CG * H + h * 2 * H, 2 * H)], ALU.mult, ALU.add)
                last.then_inc(res_ready, 1)
                if is_group(pair, n + AHEAD):
                    clip(pair, n + AHEAD)

            scale(0, 0)
            for n in range(AHEAD):
                if n < AHEAD - 1:
                    scale(0, n + 1)
                clip(0, n)
            groups(dve, group)

        @block.tensor
        def _(pe):
            PE = nc.tensor

            def keep_busy(n):
                for _ in range(n):
                    PE.matmul(p_gate[:, 0:P], ident[:, :], ident[:, :], start=True, stop=True)


            def gates_by_expert(g):
                pe.wait_ge(feat_copied, HK * (g + 1))
                if g >= 2:
                    pe.wait_ge(gateT_copied, g - 1)
                for k in range(HK):
                    last = PE.matmul(p_gateT[g % 2][0:E, :], wgf[:, k, :], x_feat[:, g % 4, k, :],
                                     start=(k == 0), stop=(k == HK - 1))
                last.then_inc(gateT_done, 1)

            def gates_by_token(g):
                pe.wait_ge(gateT_copied, g + 1)
                for c in range(g * TG // P, (g + 1) * TG // P):
                    PE.transpose(p_gate[:, c * E:(c + 1) * E], gateT[:, c * P:(c + 1) * P], ident[0:E, 0:E])

            pe.wait_ge(ident_ready, 1)
            keep_busy(5)
            for g in range(T // TG):
                pe.wait_ge(tok_in[g], 16)
                if g >= 2:
                    pe.wait_ge(feat_copied, HK * (g - 1))
                for k in range(HK):
                    for c in range(TG // P):
                        at = (g * TG // P + c) * H + k * P
                        last = PE.transpose(p_feat[g % 2][k][:, c * P:(c + 1) * P], x_tok[:, at:at + P], ident[:, :])
                    last.then_inc(feat_T, 1)
                if g < 2:
                    keep_busy(1)
                if g == 1:
                    pe.wait_ge(small_in, 16 * 6)
                    PE.matmul(p_small[0:NB, 0:E], condT_sb[:, :], gg_sb[:, :], start=True, stop=True).then_inc(cond_done, 1)
                    pe.wait_ge(wgf_ready, 1)
                elif g == 2:
                    pe.wait_ge(consts_ready, 1)
                    pe.wait_ge(fsum_ready, 1)
                    PE.matmul(p_small[:, 16:17], ones32[:, :], fsum[:, :], start=True, stop=True).then_inc(fsum_done, 1)
                if g >= 2:
                    gates_by_expert(g - 2)
                if g >= 3:
                    gates_by_token(g - 3)
            last = T // TG
            gates_by_expert(last - 2)
            gates_by_token(last - 3)
            gates_by_expert(last - 1)
            gates_by_token(last - 2)
            gates_by_token(last - 1)
            pe.wait_ge(gb_ready, 1)
            PE.matmul(p_gate[:, CW:2 * CW], batch_half[:, :], gb_col[:, :], start=True, stop=True).then_inc(gates_done, 1)
            pe.wait_ge(chosen_ready, 1)
            PE.matmul(p_rank[:, 0:CW], earlier[:, :], chosen16[:, :], start=True, stop=True)
            PE.matmul(p_total[:, 0:CW], ones16[:, :], chosen16[:, :], start=True, stop=True).then_inc(ranks_done, 1)
            pe.wait_ge(slots_ready, 1)
            keep_busy(9)
            for n, (k, part) in enumerate(halves):
                pe.wait_ge(onehots_c, n + 1)
                pe.wait_ge(onehots_p, n + 1)
                if n < len(halves) - 1:
                    pe.wait_ge(rows_ready, n + 1)
                else:
                    pe.wait_ge(last_rows, 1)
                for c in range(part.start, part.stop):
                    last = PE.matmul(p_table[:, 0:2 * NT], onehot_r[k][:, c, :],
                                     onehot_t[k][:, c, :, :].rearrange("p v t -> p (v t)"),
                                     start=(k == 0 and c == 0), stop=(k == 1 and c == C - 1))
                if n < 2:
                    keep_busy(8)
            last.then_inc(tables_done, 1)
            keep_busy(17)

            pe.wait_ge(paced, 1)
            pe.wait_ge(twos_ready, 1)

            def expert(pair, n):
                return pe.value_load(tile_e[0:1, bass.ds(2 * pair + n, 1)], min_val=0, max_val=E - 1)

            def product(psum, lhs, chunks, width, e, first, done):
                slot_at = e % RING * SLOT
                for k in range(chunks):
                    at = 2 * CH * (first + k * width // CH) + k * width % CH
                    rounded = ring[:, bass.ds(slot_at + at, width)]
                    rest = ring[:, bass.ds(slot_at + (at + CH), width)]
                    part = [t[:, k * P:(k + 1) * P] for t in lhs]
                    PE.matmul(psum[:, 0:width], part[1], rounded, start=(k == 0), stop=False)
                    PE.matmul(psum[:, 0:width], part[0], rest, start=False, stop=False)
                    last = PE.matmul(psum[:, 0:width], part[0], rounded, start=False, stop=(k == chunks - 1))
                last.then_inc(done, 1)

            def transposes(psum, src, chunks, done):
                for k in range(chunks):
                    last = PE.transpose(psum[:, k * P:(k + 1) * P], src[:, k * P:(k + 1) * P], ident[:, :])
                last.then_inc(done, 1)

            def transpose_rows(pair, n):
                pe.wait_ge(gathered[n % 2], 16 * (pair + n // 2 + 1))
                if later(pair, n, 1):
                    pe.wait_ge(xt_ready, 2 * pair + n)
                transposes(p_t0, rows[n % 2], HK, t0_done)

            def turn(pair, n, last=False):
                i, b = 2 * pair + n, n % 2
                if is_tile(pair, n, last):
                    e = expert(pair, n)
                    pe.wait_ge(chunks_done, (e + 1) * EC)
                    pe.wait_ge(xt_ready, i + 1)
                    if later(pair, n, 1):
                        pe.wait_ge(h1_ready, i)
                    product(p_l1, xt, HK, M, e, 0, l1_done)
                if is_tile(pair, n - 2, last):
                    pe.wait_ge(h2_ready, i - 1)
                    if later(pair, n, 3):
                        pe.wait_ge(h2T_ready, i - 2)
                    transposes(p_t2, h2, MK, t2_done)
                if is_tile(pair, n + 1, last):
                    transpose_rows(pair, n + 1)
                if is_tile(pair, n - 1, last):
                    e2 = expert(pair, n - 1)
                    pe.wait_ge(h1T_ready, i)
                    if later(pair, n, 2):
                        pe.wait_ge(h2_ready, i - 1)
                    product(p_l2, h1T[1 - b], MK, M, e2, W2O // CH, l2_done)
                if is_tile(pair, n, last):
                    pe.wait_ge(h1_ready, i + 1)
                    if later(pair, n, 1):
                        pe.wait_ge(h1T_ready, i)
                    transposes(p_t1, h1, MK, t1_done)
                if is_tile(pair, n - 2, last):
                    e3 = expert(pair, n - 2)
                    pe.wait_ge(h2T_ready, i - 1)
                    if later(pair, n, 3):
                        pe.wait_ge(y_ready, i - 2)
                    product(p_l3, h2T[b], MK, H, e3, W3O // CH, l3_done)

            transpose_rows(0, 0)
            turns(pe, turn)

            pe.wait_ge(low_scaled, 4)
            keep_busy(10)
            pe.wait_ge(amax_ready, 1)
            PE.transpose(p_small[0:1, 0:P], amax1[:, :], ident[:, :]).then_inc(amax_T, 1)
            pe.wait_ge(amax_one, 1)
            PE.matmul(p_small[:, 0:1], ones32[0:1, :], amax_row[:, :], start=True, stop=True).then_inc(amax_all, 1)

            def transpose_group(pair, n):
                g, b = 2 * pair + n, n % 2
                pe.wait_ge(q_ready, g + 1)
                if later(pair, n, 2):
                    pe.wait_ge(qT_ready, g - 1)
                pq = p_qT[b][:, :].bitcast(BF16)
                for j in range(CG * HK):
                    last = PE.transpose(pq[:, j * P:(j + 1) * P], q16[b][:, j * P:(j + 1) * P], ident16[:, :])
                last.then_inc(qT_done, 1)

            def group(pair, n):
                g, b = 2 * pair + n, n % 2
                if is_group(pair, n + 1):
                    transpose_group(pair, n + 1)
                pe.wait_ge(qT_ready, g + 1)
                if later(pair, n, 2):
                    pe.wait_ge(res_ready, g - 1)
                for c in range(CG):
                    for k in range(HK):
                        j = c * HK + k
                        last = PE.matmul(p_out[b][c // 2][:, (c % 2) * H:(c % 2 + 1) * H],
                                         qT[b][:, j * P:(j + 1) * P], fw_q[:, k, :],
                                         start=(k == 0), stop=(k == HK - 1))
                last.then_inc(ffn_done, 1)

            transpose_group(0, 0)
            groups(pe, group)


def kernel(x, cond_256, L0_cond_rms_w, L0_cond_wg_W, L0_cond_wg_b, L0_cond_gg_W, L0_cond_gg_b, L0_cond_W1,
           L0_cond_b1, L0_cond_W2, L0_cond_b2, L0_cond_W3, L0_cond_b3, L0_ffn_weight, L0_ffn_bias):
    import numpy as np
    import concourse.bacc as bacc
    from concourse.bass_utils import run_bass_kernel_spmd

    def np_(a):
        return np.asarray(a)

    x_rows = np_(x).reshape(-1, np_(x).shape[-1])
    E = np_(L0_cond_W1).shape[0]

    def chunks(a):
        a = np_(a)
        return a.reshape(E, a.shape[1] // 128, 128, a.shape[2]).transpose(2, 0, 1, 3).reshape(128, E, -1)

    arrays = {
        "x": x_rows,
        "condT": np_(cond_256).reshape(-1, 2, np_(cond_256).shape[-1]).transpose(2, 1, 0).reshape(np_(cond_256).shape[-1], -1),
        "rms": np_(L0_cond_rms_w).reshape(-1, 128).T,
        "wg": np_(L0_cond_wg_W), "wgb": np_(L0_cond_wg_b), "gg": np_(L0_cond_gg_W), "ggb": np_(L0_cond_gg_b),
        "w": np.concatenate([chunks(L0_cond_W1), chunks(L0_cond_W2), chunks(L0_cond_W3)], axis=2).reshape(128, -1),
        "b1": np_(L0_cond_b1), "b2": np_(L0_cond_b2), "b3": np_(L0_cond_b3),
        "fwT": np_(L0_ffn_weight).T, "fbias": np_(L0_ffn_bias),
    }
    arrays = {name: np.ascontiguousarray(a) for name, a in arrays.items()}
    nc = bacc.Bacc("TRN2", target_bir_lowering=False, num_devices=1)
    args = {name: nc.dram_tensor(f"in_{name}", a.shape, mybir.dt.from_np(a.dtype), kind="ExternalInput").ap()
            for name, a in arrays.items()}
    out = nc.dram_tensor("out_0", x_rows.shape, F32, kind="ExternalOutput").ap()
    moe_ffn(nc, out=out, **args)
    r = run_bass_kernel_spmd(nc, [{f"in_{name}": a for name, a in arrays.items()}], core_ids=[0])
    return r.results[0]["out_0"].reshape(np_(x).shape)
```
